# Optimizing a Trainium2 kernel written in Bass

```python
import numpy as np
import jax
import jax.numpy as jnp

def _softmax(x, axis=-1):
    return jax.nn.softmax(x, axis=axis)

def _gelu(x):
    return jax.nn.gelu(x, approximate=True)

def _silu(x):
    return jax.nn.silu(x)

def _sigmoid(x):
    return jax.nn.sigmoid(x)

def _layernorm(x, axis=-1, eps=1e-05):
    m = jnp.mean(x, axis=axis, keepdims=True)
    v = jnp.var(x, axis=axis, keepdims=True)
    return (x - m) / jnp.sqrt(v + eps)

def _scatter_add(tgt, idx, src, axis=0):
    return tgt.at[idx].add(src)

def _segment_sum(src, seg, n):
    return jax.ops.segment_sum(src, seg, n)
kernel_name = 'mk_prb_d1_jaxref_r8_0a79ff'

def setup_inputs(seed: int=0):
    np.random.seed(seed)
    _w = jnp.asarray

    def _L0_attn_setup():
        import jax, jax.numpy as jnp
        import numpy as np
        D_MODEL = 128
        N_HEADS = 16
        D_HEAD = 64
        LAMBDA_INIT = 0.8
        key = jax.random.key(seed)
        ks = jax.random.split(key, 6)
        B, S = (2, 256)
        std = 0.02
        x = jax.random.normal(ks[0], (B, S, D_MODEL), dtype=jnp.float32)
        Wq = jax.random.normal(ks[1], (D_MODEL, 2 * N_HEADS * D_HEAD), dtype=jnp.float32) * std
        Wk = jax.random.normal(ks[2], (D_MODEL, 2 * N_HEADS * D_HEAD), dtype=jnp.float32) * std
        Wv = jax.random.normal(ks[3], (D_MODEL, 2 * N_HEADS * D_HEAD), dtype=jnp.float32) * std
        Wo = jax.random.normal(ks[4], (N_HEADS * D_HEAD, D_MODEL), dtype=jnp.float32) * std
        lq1 = jnp.zeros((D_HEAD,), dtype=jnp.float32)
        lk1 = jnp.zeros((D_HEAD,), dtype=jnp.float32)
        lq2 = jnp.zeros((D_HEAD,), dtype=jnp.float32)
        lk2 = jnp.zeros((D_HEAD,), dtype=jnp.float32)
        return {'x': x, 'Wq': Wq, 'Wk': Wk, 'Wv': Wv, 'Wo': Wo, 'lq1': lq1, 'lk1': lk1, 'lq2': lq2, 'lk2': lk2}
    _L0_attn_in = _L0_attn_setup()

    def _L0_ffn_setup():
        import jax, jax.numpy as jnp
        import numpy as np
        T, Z, D_DIM = (8, 256, 128)
        N_EXP, P_SLOT, H = (64, 32, 128)
        LN_EPS = 1e-05
        key = jax.random.key(seed)
        k = jax.random.split(key, 5)
        s = 0.02
        return {'x': jax.random.normal(k[0], (T, Z, D_DIM), dtype=jnp.float32), 'phi_w': jax.random.normal(k[1], (N_EXP * P_SLOT, D_DIM), dtype=jnp.float32) * s, 'phi_b': jax.random.normal(k[2], (N_EXP * P_SLOT,), dtype=jnp.float32) * s, 'expert_w': jax.random.normal(k[3], (N_EXP, D_DIM, H), dtype=jnp.float32) * s, 'expert_b': jax.random.normal(k[4], (N_EXP, H), dtype=jnp.float32) * s}
    _L0_ffn_in = _L0_ffn_setup()
    _d = {'L0_attn_x': _L0_attn_in['x'], 'L0_attn_Wq': _L0_attn_in['Wq'], 'L0_attn_Wk': _L0_attn_in['Wk'], 'L0_attn_Wv': _L0_attn_in['Wv'], 'L0_attn_Wo': _L0_attn_in['Wo'], 'L0_attn_lq1': _L0_attn_in['lq1'], 'L0_attn_lk1': _L0_attn_in['lk1'], 'L0_attn_lq2': _L0_attn_in['lq2'], 'L0_attn_lk2': _L0_attn_in['lk2'], 'L0_ffn_phi_w': _L0_ffn_in['phi_w'], 'L0_ffn_phi_b': _L0_ffn_in['phi_b'], 'L0_ffn_expert_w': _L0_ffn_in['expert_w'], 'L0_ffn_expert_b': _L0_ffn_in['expert_b']}
    _x0 = _d['L0_attn_x']
    _d['L0_attn_x'] = jax.random.normal(jax.random.fold_in(jax.random.key(seed), 1), (16, 256, 128), dtype=_x0.dtype)
    del _x0
    return _d

def reference(L0_attn_x, L0_attn_Wq, L0_attn_Wk, L0_attn_Wv, L0_attn_Wo, L0_attn_lq1, L0_attn_lk1, L0_attn_lq2, L0_attn_lk2, L0_ffn_phi_w, L0_ffn_phi_b, L0_ffn_expert_w, L0_ffn_expert_b):

    def _L0_attn_ref(x, Wq, Wk, Wv, Wo, lq1, lk1, lq2, lk2):
        import jax, jax.numpy as jnp
        import numpy as np
        D_MODEL = 128
        N_HEADS = 16
        D_HEAD = 64
        LAMBDA_INIT = 0.8
        B, S, D = x.shape
        h, dh = (N_HEADS, D_HEAD)
        q = (x @ Wq).reshape(B, S, 2, h, dh)
        k = (x @ Wk).reshape(B, S, 2, h, dh)
        v = (x @ Wv).reshape(B, S, 2, h, dh)
        q1, q2 = (q[:, :, 0], q[:, :, 1])
        k1, k2 = (k[:, :, 0], k[:, :, 1])
        v1, v2 = (v[:, :, 0], v[:, :, 1])
        scale = 1.0 / jnp.sqrt(jnp.asarray(dh, dtype=x.dtype))
        lam = jnp.exp(jnp.dot(lq1, lk1)) - jnp.exp(jnp.dot(lq2, lk2)) + LAMBDA_INIT
        causal = jnp.tril(jnp.ones((S, S), dtype=bool))
        neg_inf = jnp.asarray(-1e+30, dtype=x.dtype)
        s1 = jnp.einsum('bshd,bthd->bhst', q1, k1) * scale
        s2 = jnp.einsum('bshd,bthd->bhst', q2, k2) * scale
        s1 = jnp.where(causal, s1, neg_inf)
        s2 = jnp.where(causal, s2, neg_inf)
        a1 = jax.nn.softmax(s1, axis=-1)
        a2 = jax.nn.softmax(s2, axis=-1)
        o = jnp.einsum('bhst,bthd->bshd', a1, v1) - lam * jnp.einsum('bhst,bthd->bshd', a2, v2)
        o = o.reshape(B, S, h * dh) * (1.0 - LAMBDA_INIT)
        return o @ Wo

    def _L0_ffn_ref(x, phi_w, phi_b, expert_w, expert_b):
        import jax, jax.numpy as jnp
        import numpy as np
        T, Z, D_DIM = (8, 256, 128)
        N_EXP, P_SLOT, H = (64, 32, 128)
        LN_EPS = 1e-05
        t, z, d = x.shape
        n = expert_w.shape[0]
        p = phi_w.shape[0] // n
        logits = (jnp.einsum('tzd,ed->tze', x, phi_w) + phi_b).reshape(t, z, n, p)
        D = jax.nn.softmax(logits, axis=3)
        C = jax.nn.softmax(logits, axis=2)
        X_tilde = jnp.einsum('tznp,tzd->npd', D, x)
        X_tilde = jnp.clip(X_tilde, -33000.0, 65000.0)
        mu = jnp.mean(X_tilde, axis=-1, keepdims=True)
        var = jnp.mean(jnp.square(X_tilde - mu), axis=-1, keepdims=True)
        X_tilde = (X_tilde - mu) * jax.lax.rsqrt(var + LN_EPS)
        X_tilde = jnp.tanh(X_tilde)
        Y_tilde = jnp.einsum('npd,ndH->npH', X_tilde, expert_w) + expert_b[:, None, :]
        Y = jnp.einsum('tznp,npH->tzH', C, Y_tilde)
        return Y
    x = L0_attn_x
    xn = _layernorm(x, axis=-1)
    x = x + _L0_attn_ref(xn, L0_attn_Wq, L0_attn_Wk, L0_attn_Wv, L0_attn_Wo, L0_attn_lq1, L0_attn_lk1, L0_attn_lq2, L0_attn_lk2) + _L0_ffn_ref(xn, L0_ffn_phi_w, L0_ffn_phi_b, L0_ffn_expert_w, L0_ffn_expert_b)
    return x

_drawn_inputs = setup_inputs


def setup_inputs(seed=0):
    import zlib

    import numpy as np

    out = dict(_drawn_inputs(seed))
    spreads = {'L0_attn_lq1': (0.0, 2.0),
     'L0_attn_lk1': (0.0, 2.0),
     'L0_attn_lq2': (0.0, 0.8),
     'L0_attn_lk2': (0.0, 0.8)}
    factors = {'L0_attn_Wq': 8.0,
     'L0_attn_Wk': 8.0,
     'L0_attn_Wv': 8.0,
     'L0_attn_Wo': 8.0,
     'L0_ffn_phi_b': 64.0,
     'L0_ffn_phi_w': 8.0,
     'L0_ffn_expert_w': 8.0,
     'L0_ffn_expert_b': 55.394}
    for name, (base, spread) in spreads.items():
        noise = np.random.default_rng([zlib.crc32(name.encode()), seed]).standard_normal(out[name].shape)
        drawn = base * np.exp(spread * noise) if base else spread * noise
        out[name] = jnp.asarray(drawn.astype(out[name].dtype))
    for name, factor in factors.items():
        out[name] = (out[name] * factor).astype(out[name].dtype)
    return out
```

```python
from contextlib import ExitStack

import numpy as np

import concourse.bass as bass
from concourse import mybir
from concourse.alu_op_type import AluOpType as ALU

F32 = mybir.dt.float32
F32R = mybir.dt.float32r
BF16 = mybir.dt.bfloat16
ACT = mybir.ActivationFunctionType
AX = mybir.AxisListType

P = 128
NB, S, D = 16, 256, 128
NT = NB * S
NTT = NT // P
DH = 64
NH = 16
NHH = 2 * NH
G = 4
NG = NHH // G
NPAIR = NB // 2
PT = 2 * S
NU = NG * NPAIR
NV = 2 * NU
NE, NP_, NS_ = 64, 32, 2048
NST = NS_ // P
BK = 512
LAMBDA_INIT = 0.8
OUT_SCALE = 1.0 - LAMBDA_INIT
SCORE_SCALE = DH ** -0.5
EPS = 1e-5
MASKED = -1e30
ITER = NTT


def wait(eng, sem, value):
    if isinstance(value, int) and value <= 0:
        return
    eng.wait_ge(sem, value)


def live(i, n):
    return not isinstance(i, int) or 0 <= i < n


def f32(ap):
    return ap.bitcast(F32)


def product3(pe, out, w_hi, w_lo, m_hi, m_lo, start=True, stop=True):
    pe.matmul(out, w_hi, m_hi, start=start, stop=False, skip_group_check=True)
    pe.matmul(out, w_hi, m_lo, start=False, stop=False, skip_group_check=True)
    return pe.matmul(out, w_lo, m_hi, start=False, stop=stop, skip_group_check=True)


def setup_phase(nc, env):
    NBANK = 6
    with ExitStack() as ctx:
        def sb(name, shape, dt=F32):
            return ctx.enter_context(nc.sbuf_tensor(name, shape, dt))

        def sem(name):
            return ctx.enter_context(nc.semaphore(name))

        x_sb = sb("x_sb", [P, NTT, D])
        wq, wk, wv = (sb(n, [P, NHH * DH]) for n in ("wq", "wk", "wv"))
        wo = sb("wo", [P, NH // 2, D])
        phi_w = sb("phi_w", [P, NST, D])
        wT = {n: sb(n + "T", [P, NHH * DH]) for n in ("wq", "wk", "wv")}
        stage = sb("stage", [P, 4, 2, BK], F32R)
        lqk = sb("lqk", [P, 4, DH])
        lprod = sb("lprod", [P, 2, DH])
        ldot = sb("ldot", [P, 2])
        lexp = sb("lexp", [P, 2])
        lam = sb("lam", [P, 1])
        neg_lam = sb("neg_lam", [P, 1])
        stats = sb("stats", [P, NTT, 6])
        mv = sb("mv", [P, NTT, 2])
        var = sb("var", [P, NTT])
        root = sb("root", [P, NTT])
        rstd = sb("rstd", [P, NTT])
        quot = sb("quot", [P, NTT])
        phib_rows = sb("phib_rows", [NST, P])
        ps = ctx.enter_context(nc.psum_tensor("ps_setup", [P, NBANK, BK], F32))
        ps_b = ctx.enter_context(nc.psum_tensor("ps_phib", [P, BK], F32))

        loaded = {n: sem("loaded_" + n) for n in ("x", "phi", "wq", "wk", "wv", "wo", "l", "phib")}
        s_const = sem("s_const")
        job_done = sem("job_done")
        hi_out = sem("hi_out")
        lo_out = sem("lo_out")
        ln_step = sem("ln_step")
        var_root = sem("var_root")
        xn_ready = sem("xn_ready")
        lam_step = sem("lam_step")
        lam_exp = sem("lam_exp")
        ab_stored = [sem(f"ab_stored{i}") for i in range(4)]
        xn_stored = sem("xn_stored")
        phib_done = sem("phib_done")
        phib_out = sem("phib_out")

        ident, identb, mask = env["ident"], env["identb"], env["mask"]
        xT, phiT = env["xT"], env["phiT"]
        ab_dram, xn_dram = env["ab_dram"], env["xn_dram"]

        jobs = [("phi", i) for i in range(4)] + [("x", i) for i in range(8)]
        jobs += [("wq", i) for i in range(4)] + [("wk", i) for i in range(4)] + [("A", i) for i in range(NG)]
        jobs += [("wv", i) for i in range(4)] + [("B", i) for i in range(NG)]
        SPLIT = ("phi", "x", "A", "B")
        lo_count = [sum(k in SPLIT for k, _ in jobs[:n + 1]) for n in range(len(jobs))]
        at = {job: n for n, job in enumerate(jobs)}
        ab_jobs = [j for j in jobs if j[0] in "AB"]
        ab_index = {j: i for i, j in enumerate(ab_jobs)}

        def parts(kind, i):
            if kind == "phi":
                return [t[:, i * BK:(i + 1) * BK] for t in phiT]
            if kind == "x":
                return [t[:, i * BK:(i + 1) * BK] for t in xT]
            slot = ab_index[(kind, i)] % 4
            return [stage[:, slot, h, :] for h in range(2)]

        block = ctx.enter_context(nc.Block())

        @block.sync
        def _(sp):
            sp.dma_start(x_sb[:], env["x"].rearrange("(t p) d -> p t d", p=P)).then_inc(loaded["x"], 16)
            sp.dma_start(phi_w[:], env["phi_w"].rearrange("(t p) d -> p t d", p=P)).then_inc(loaded["phi"], 16)
            for i, v in enumerate(("lq1", "lk1", "lq2", "lk2")):
                sp.dma_start(lqk[:, i, :], env[v].partition_broadcast(P)).then_inc(loaded["l"], 16)
            sp.dma_start(wv[:], env["wv"]).then_inc(loaded["wv"], 16)
            sp.dma_start(wo[:], env["wo"].rearrange("(t p) d -> p t d", p=P)).then_inc(loaded["wo"], 16)
            sp.wait_ge(xn_ready, 1)
            sp.dma_start(xn_dram.rearrange("t p d -> p t d"), x_sb[:]).then_inc(xn_stored, 16)
            for n, (kind, i) in enumerate(ab_jobs):
                sp.wait_ge(hi_out, at[(kind, i)] + 1)
                sp.wait_ge(lo_out, lo_count[at[(kind, i)]])
                sp.dma_start(ab_dram["AB".index(kind), i].rearrange("h p n -> p h n"),
                             f32(stage[:, n % 4])).then_inc(ab_stored[n % 4], 16)
            for q in range(4):
                sp.wait_ge(ab_stored[q], 16 * len(ab_jobs) // 4)
            sp.wait_ge(xn_stored, 16)

        @block.gpsimd
        def _(pool):
            for t in (ident, identb):
                nc.gpsimd.memset(t[:], 0.0).then_inc(s_const, 1)
            nc.gpsimd.memset(mask[:], 0.0).then_inc(s_const, 1)
            pool.wait_ge(s_const, 3)
            for t in (ident, identb):
                nc.gpsimd.affine_select(out=t[:], in_=t[:], compare_op=ALU.not_equal, fill=1.0, base=0,
                                        pattern=[[-1, P]], channel_multiplier=1).then_inc(s_const, 1)
            nc.gpsimd.affine_select(out=mask[:], in_=mask[:], compare_op=ALU.is_ge, fill=MASKED, base=0,
                                    pattern=[[0, G], [-1, P]], channel_multiplier=1).then_inc(s_const, 1)
            nc.gpsimd.memset(env["o_acc"][:], 0.0)
            nc.gpsimd.memset(env["xt_acc"][:], 0.0)
            nsel = env["nsel_f"]
            nc.gpsimd.memset(nsel[:], 0.0).then_inc(s_const, 1)
            pool.wait_ge(s_const, 7)
            for n, base in enumerate((0, -NP_)):
                nc.gpsimd.affine_select(out=nsel[:], in_=nsel[:], compare_op=ALU.not_equal, fill=-1.0, base=base,
                                        pattern=[[0, P // NP_], [-1, NP_]], channel_multiplier=1).then_inc(s_const, 1)
                pool.wait_ge(s_const, 8 + n)

        @block.scalar
        def _(act):
            act.dma_start(wq[:], env["wq"]).then_inc(loaded["wq"], 16)
            act.dma_start(wk[:], env["wk"]).then_inc(loaded["wk"], 16)
            act.dma_start(phib_rows[:], env["phi_b"].rearrange("(t p) -> t p", p=P)).then_inc(loaded["phib"], 16)
            act.wait_ge(ln_step, 1)
            nc.scalar.activation(root[:], var[:], ACT.Sqrt).then_inc(var_root, 1)
            act.wait_ge(lam_step, 2)
            nc.scalar.activation(lexp[:], ldot[:], ACT.Exp).then_inc(lam_exp, 1)
            act.wait_ge(phib_done, 1)
            nc.scalar.activation(env["phibT"][:], ps_b[:, 0:NST], ACT.Copy).then_inc(phib_out, 1)
            for n, (kind, i) in enumerate(jobs):
                bank = ps[:, n % NBANK, :]
                act.wait_ge(job_done, n + 1)
                if kind in SPLIT:
                    if kind in "AB" and ab_index[(kind, i)] >= 4:
                        act.wait_ge(ab_stored[ab_index[(kind, i)] % 4], 16 * (ab_index[(kind, i)] // 4))
                    hi = parts(kind, i)[0]
                    if kind == "A":
                        nc.scalar.activation(hi, bank, ACT.Copy, scale=SCORE_SCALE).then_inc(hi_out, 1)
                    elif kind == "B" and i < NG // 2:
                        nc.scalar.activation(hi, bank, ACT.Copy, scale=OUT_SCALE).then_inc(hi_out, 1)
                    elif kind == "B":
                        act.wait_ge(lam_step, 4)
                        nc.scalar.activation(hi, bank, ACT.Identity, scale=neg_lam[:]).then_inc(hi_out, 1)
                    else:
                        nc.scalar.activation(hi, bank, ACT.Copy).then_inc(hi_out, 1)
                else:
                    nc.scalar.activation(wT[kind][:, i * BK:(i + 1) * BK], bank, ACT.Copy).then_inc(hi_out, 1)

        @block.vector
        def _(dve):
            dve.wait_ge(loaded["x"], 16)
            for t in range(NTT):
                nc.vector.bn_stats(stats[:, t, :], x_sb[:, t, :])
            dve.drain()
            for t in range(NTT):
                nc.vector.bn_aggr(mv[:, t, :], stats[:, t, :])
            dve.drain()
            nc.vector.tensor_scalar(var[:], mv[:, :, 1], EPS, None, ALU.add).then_inc(ln_step, 1)
            dve.wait_ge(var_root, 1)
            nc.vector.reciprocal(quot[:], root[:]).then_inc(ln_step, 1)
            dve.wait_ge(ln_step, 2)
            nc.vector.tensor_tensor(quot[:], quot[:], var[:], ALU.mult).then_inc(ln_step, 1)
            dve.wait_ge(ln_step, 3)
            nc.vector.tensor_tensor(quot[:], quot[:], root[:], ALU.add).then_inc(ln_step, 1)
            dve.wait_ge(ln_step, 4)
            nc.vector.tensor_scalar(quot[:], quot[:], 0.5, None, ALU.mult).then_inc(ln_step, 1)
            dve.wait_ge(ln_step, 5)
            nc.vector.reciprocal(rstd[:], quot[:]).then_inc(ln_step, 1)
            dve.wait_ge(ln_step, 6)
            for t in range(NTT):
                last = nc.vector.tensor_scalar(x_sb[:, t, :], x_sb[:, t, :], mv[:, t, 0:1], rstd[:, t:t + 1],
                                               ALU.subtract, ALU.mult)
            last.then_inc(xn_ready, 1)
            dve.wait_ge(loaded["l"], 64)
            nc.vector.tensor_tensor(lprod[:], lqk[:, 0:4:2, :], lqk[:, 1:4:2, :], ALU.mult).then_inc(lam_step, 1)
            dve.wait_ge(lam_step, 1)
            nc.vector.tensor_reduce(ldot[:], lprod[:], AX.X, ALU.add).then_inc(lam_step, 1)
            dve.wait_ge(lam_exp, 1)
            nc.vector.tensor_tensor(lam[:], lexp[:, 0:1], lexp[:, 1:2], ALU.subtract).then_inc(lam_step, 1)
            dve.wait_ge(lam_step, 3)
            nc.vector.tensor_scalar(neg_lam[:], lam[:], LAMBDA_INIT, -OUT_SCALE, ALU.add, ALU.mult).then_inc(lam_step, 1)
            dve.wait_ge(lam_step, 4)
            dve.wait_ge(s_const, 9)
            nc.vector.tensor_copy(env["nsel"][:], env["nsel_f"][:])
            for n, (kind, i) in enumerate(jobs):
                if kind not in SPLIT:
                    continue
                hi, lo = parts(kind, i)
                scale = {"A": SCORE_SCALE, "B": OUT_SCALE if i < NG // 2 else neg_lam[:]}.get(kind, 1.0)
                dve.wait_ge(hi_out, n + 1)
                nc.vector.scalar_tensor_tensor(out=lo, in0=ps[:, n % NBANK, :], scalar=scale, in1=f32(hi),
                                               op0=ALU.mult, op1=ALU.subtract).then_inc(lo_out, 1)

        @block.tensor
        def _(pe):
            pe.wait_ge(s_const, 6)
            pe.wait_ge(loaded["phib"], 16)
            pe.transpose(ps_b[:, 0:NST], phib_rows[:], ident[0:NST, 0:NST]).then_inc(phib_done, 1)
            need = {"phi": "phi", "wq": "wq", "wk": "wk", "wv": "wv", "B": "wo"}
            for n, (kind, i) in enumerate(jobs):
                if n >= NBANK:
                    pe.wait_ge(hi_out, n - NBANK + 1)
                    wait(pe, lo_out, lo_count[n - NBANK])
                if kind in need and i == 0:
                    pe.wait_ge(loaded[need[kind]], 16)
                if kind == "x" and i == 0:
                    pe.wait_ge(xn_ready, 1)
                if kind in "AB" and i == 0:
                    pe.wait_ge(hi_out, at[("wk" if kind == "A" else "wv", 3)] + 1)
                for j in range(4):
                    out = ps[:, n % NBANK, j * P:(j + 1) * P]
                    c = 4 * i + j
                    if kind == "phi":
                        mm = pe.transpose(out, phi_w[:, c, :], ident[:])
                    elif kind == "x":
                        mm = pe.transpose(out, x_sb[:, c, :], ident[:])
                    elif kind in wT:
                        src = {"wq": wq, "wk": wk, "wv": wv}[kind]
                        mm = pe.transpose(out, src[:, c * P:(c + 1) * P], ident[:])
                    else:
                        c = 8 * (i // 2) + 2 * j + i % 2
                        r0, t0 = (c % 2) * DH, (c // 2) * P
                        rows = slice(r0, r0 + DH)
                        if kind == "A":
                            mm = pe.matmul(out, wT["wk"][rows, t0:t0 + P], wT["wq"][rows, t0:t0 + P],
                                           start=True, stop=True, skip_group_check=True)
                        else:
                            mm = pe.matmul(out, wT["wv"][rows, t0:t0 + P], wo[rows, (c // 2) % (NH // 2), :],
                                           start=True, stop=True, skip_group_check=True)
                mm.then_inc(job_done, 1)


def main_phase(nc, env):
    with ExitStack() as ctx:
        def sb(name, shape, dt=F32):
            return ctx.enter_context(nc.sbuf_tensor(name, shape, dt))

        def psum(name, banks):
            return ctx.enter_context(nc.psum_tensor(name, [P, banks, BK], F32))

        def sem(name):
            return ctx.enter_context(nc.semaphore(name))

        xs = [[sb(f"xs{q}{h}", [P, PT], F32R) for h in range(2)] for q in range(2)]
        a_w = [sb(f"a_w{h}", [P, G * P], F32R) for h in range(2)]
        b_w = [sb(f"b_w{h}", [P, G * P], F32R) for h in range(2)]
        tp = [sb(f"tp{h}", [P, G, PT], F32R) for h in range(2)]
        u = [sb(f"u{q}", [P, 4, G * P]) for q in range(2)]
        e0 = [sb(f"e0{q}", [P, G, P]) for q in range(2)]
        e1 = [sb(f"e1{q}", [P, G, S]) for q in range(2)]
        pT = sb("pT", [P, 3, BK])
        neg_max = sb("neg_max", [P, 2, 2 * G])
        total = sb("total", [P, 2, 2 * G])
        inv = sb("inv", [P, 2, 2 * G])
        fx = [sb(f"fx{h}", [P, P], F32R) for h in range(2)]
        fxn = sb("fxn", [P, D])
        bias = sb("bias", [P, NS_])
        logit = sb("logit", [P, 2 * NS_])
        disp = sb("disp", [P, 2 * NS_])
        gmax = sb("gmax", [P, NE])
        dsum = sb("dsum", [P, NE])
        dinv = sb("dinv", [P, NE])
        spare = sb("spare", [P, 1])
        ps_tu, ps_s, ps_t, ps_o = psum("ps_tu", 2), psum("ps_s", 3), psum("ps_t", 2), psum("ps_o", 1)

        xs_in = [sem("xs_in0"), sem("xs_in1")]
        a_in, b_in, fx_in, fxn_in, bias_in = (sem(n) for n in ("a_in", "b_in", "fx_in", "fxn_in", "bias_in"))
        tp_mm, u_mm, lg_mm, xt_mm, s_mm, t_mm, av_mm = (
            sem(n) for n in ("tp_mm", "u_mm", "lg_mm", "xt_mm", "s_mm", "t_mm", "av_mm"))
        tp_hi, tp_lo, u_out, lg_out, xt_out, t_out, o_out = (
            sem(n) for n in ("tp_hi", "tp_lo", "u_out", "lg_out", "xt_out", "t_out", "o_out"))
        max_done, exp_done, inv_done, norm_done = (sem(n) for n in ("max_done", "exp_done", "inv_done", "norm_done"))
        g_done, d_sub, d_exp, d_sum, d_inv, d_norm = (
            sem(n) for n in ("g_done", "d_sub", "d_exp", "d_sum", "d_inv", "d_norm"))
        m_done, c_sub, c_exp, c_sum = (sem(n) for n in ("m_done", "c_sub", "c_exp", "c_sum"))

        ident, identb, mask = env["ident"], env["identb"], env["mask"]
        xT, phiT, o_acc, xt_acc = env["xT"], env["phiT"], env["o_acc"], env["xt_acc"]
        m_all, c_all = env["m_all"], env["c_all"]
        ab_dram, xn_dram = env["ab_dram"], env["xn_dram"]

        block = ctx.enter_context(nc.Block())

        def run(eng, step):
            for it in range(3):
                for j in range(4):
                    step(it, j)
            with eng.Fori(3, ITER - 1) as it:
                for j in range(4):
                    step(it, j)
            for it in range(ITER - 1, ITER + 2):
                for j in range(4):
                    step(it, j)

        @block.sync
        def _(sp):
            def load_xs(unit, q, pair):
                if not live(unit, NU):
                    return
                wait(sp, s_mm, 3 * (2 * (unit - 2) + 2))
                wait(sp, u_mm, 4 * (unit - 1))
                for h in range(2):
                    sp.dma_start(f32(xs[q][h][:]), f32(xT[h][:, bass.ds(pair * PT, PT)])).then_inc(xs_in[q], 16)

            def load_group(g, w, kind, count, s_in):
                wait(sp, count, G * NPAIR * g)
                for h in range(2):
                    sp.dma_start(f32(w[h][:]), ab_dram[kind, g, h]).then_inc(s_in, 16)

            def load_tile(t):
                if live(t, NTT):
                    wait(sp, lg_mm, 4 * t)
                    for h in range(2):
                        sp.dma_start(f32(fx[h][:]), f32(xT[h][:, bass.ds(t * P, P)])).then_inc(fx_in, 16)

            def load_tokens(t):
                if live(t, NTT):
                    wait(sp, xt_mm, 4 * t)
                    sp.dma_start(fxn[:], xn_dram[t]).then_inc(fxn_in, 16)

            def iteration(it, kk, g_next=None):
                load_xs(2 * it + 2, 0, (2 * kk + 2) % NPAIR)
                if g_next is not None:
                    load_group(g_next, a_w, 0, tp_mm, a_in)
                    load_group(g_next, b_w, 1, u_mm, b_in)
                load_xs(2 * it + 3, 1, (2 * kk + 3) % NPAIR)
                load_tile(it + 1)
                load_tokens(it - 1)

            per = NPAIR // 2
            load_group(0, a_w, 0, tp_mm, a_in)
            load_xs(0, 0, 0)
            load_group(0, b_w, 1, u_mm, b_in)
            load_xs(1, 1, 1)
            load_tile(0)
            sp.dma_start(bias[:], env["phi_b"].partition_broadcast(P)).then_inc(bias_in, 16)
            for it in range(per):
                iteration(it, it % per, 1 if it == per - 1 else None)
            with sp.Fori(1, NG - 1) as g:
                for kk in range(per):
                    iteration(g * per + kk, kk, g + 1 if kk == per - 1 else None)
            for it in range(ITER - per, ITER + 1):
                iteration(it, it % per)

        @block.tensor
        def _(pe):
            def transposes(v, q, ks):
                if ks[0] == 0:
                    pe.wait_ge(norm_done, v + 1)
                for k in ks:
                    n = 3 * v + k
                    bank = ps_t[:, (q + k) % 2, :]
                    wait(pe, t_out, n - 1)
                    for i in range(4):
                        if k == 2:
                            src = e1[q][:, i, P:S]
                        elif i % 2 == 0:
                            src = e0[q][:, 2 * k + i // 2, :]
                        else:
                            src = e1[q][:, 2 * k + i // 2, 0:P]
                        mm = pe.transpose(bank[:, i * P:(i + 1) * P], src, ident[:])
                    mm.then_inc(t_mm, 1)

            def scores(v, j, unit, ks):
                b, q = j % 2, (j // 2) % 2
                if b == 0 and ks[0] == 0:
                    pe.wait_ge(tp_hi, G * (unit + 1))
                    pe.wait_ge(tp_lo, G * (unit + 1))
                c0 = b * S
                for k in ks:
                    wait(pe, exp_done, 3 * (v - 1) + k + 1)
                    bank = ps_s[:, k, :]
                    if k == 0:
                        w, m = slice(c0, c0 + P), (slice(0, G), slice(c0, c0 + P))
                        masked, heads = bank.rearrange("p (h t) -> p h t", h=G), G
                        out = masked
                    else:
                        w, m = slice(c0 + P, c0 + S), (slice(2 * k - 2, 2 * k), slice(c0, c0 + S))
                        out = bank.rearrange("p (h t) -> p h t", h=2)
                        masked, heads = out[:, :, P:S], 2
                    product3(pe, out, xs[q][0][:, w], xs[q][1][:, w], tp[0][:, m[0], m[1]], tp[1][:, m[0], m[1]],
                             stop=False)
                    pe.matmul(masked, identb[:], mask[:, 0:heads, :], start=False, stop=True,
                              skip_group_check=True).then_inc(s_mm, 1)

            def logits(t, j):
                pe.wait_ge(fx_in, 32 * (t + 1))
                product3(pe, ps_tu[:, 0, :], fx[0][:], fx[1][:], phiT[0][:, j * BK:(j + 1) * BK],
                         phiT[1][:, j * BK:(j + 1) * BK]).then_inc(lg_mm, 1)

            def dispatch(t, j):
                if j == 0:
                    pe.wait_ge(fxn_in, 16 * (t + 1))
                    pe.wait_ge(d_norm, t + 1)
                if not live(t + 2, NTT):
                    wait(pe, xt_out, 4 * t + j)
                pe.matmul(ps_tu[:, 1, :], fxn[:], disp[:, bass.ds((t % 2) * NS_ + j * BK, BK)],
                          start=True, stop=True).then_inc(xt_mm, 1)

            def output(v, j, unit, part):
                b, q = j % 2, (j // 2) % 2
                if part == 0 and b == 0:
                    pe.wait_ge(u_out, 4 * (unit + 1))
                    wait(pe, o_out, unit)
                for i in range(G):
                    if part == 0:
                        if i % 2 == 0:
                            pe.wait_ge(t_out, 3 * v + i // 2 + 1)
                        mm = pe.matmul(ps_o[:, 0, b * S:(b + 1) * S], u[q][:, 2 * b, i * P:(i + 1) * P],
                                       pT[:, i // 2, (i % 2) * S:(i % 2 + 1) * S],
                                       start=(b == 0 and i == 0), stop=False, skip_group_check=True)
                    else:
                        if i == 0:
                            pe.wait_ge(t_out, 3 * v + 3)
                        mm = pe.matmul(ps_o[:, 0, b * S + P:(b + 1) * S], u[q][:, 2 * b + 1, i * P:(i + 1) * P],
                                       pT[:, 2, i * P:(i + 1) * P], start=False, stop=(i == G - 1),
                                       skip_group_check=True)
                if part == 1:
                    mm.then_inc(av_mm, 1)

            def make_tp(unit, q, g, jobs=range(G)):
                for i in jobs:
                    if i == 0:
                        pe.wait_ge(a_in, 32 * (g + 1))
                        pe.wait_ge(xs_in[q], 32 * (unit // 2 + 1))
                    ring_free(i, unit, tp=True)
                    product3(pe, ps_tu[:, i % 2, :], a_w[0][:, i * P:(i + 1) * P], a_w[1][:, i * P:(i + 1) * P],
                             xs[q][0][:], xs[q][1][:]).then_inc(tp_mm, 1)

            def make_u(unit, q, g, jobs=range(4)):
                for i in jobs:
                    if i == 0:
                        pe.wait_ge(b_in, 32 * (g + 1))
                    ring_free(i, unit, tp=False)
                    product3(pe, ps_tu[:, i % 2, :], xs[q][0][:, i * P:(i + 1) * P], xs[q][1][:, i * P:(i + 1) * P],
                             b_w[0][:], b_w[1][:]).then_inc(u_mm, 1)

            state = {}

            def ring_free(i, unit, tp):
                if i == 0:
                    wait(pe, lg_out, state["lg"])
                elif i == 1:
                    wait(pe, xt_out, state["xt"])
                elif tp:
                    pe.wait_ge(tp_hi, G * unit + i - 1)
                    pe.wait_ge(tp_lo, G * unit + i - 1)
                else:
                    pe.wait_ge(u_out, 4 * unit + i - 1)

            def step(it, j):
                v = 4 * it + j
                unit = 2 * it + j // 2
                for ks in ((0, 1), (2,)):
                    if live(v - 2, NV):
                        transposes(v - 2, j % 2, ks)
                    if live(v, NV):
                        scores(v, j, unit, (0,) if ks[0] == 0 else (1, 2))
                if j % 2 == 0:
                    made = unit if not isinstance(unit, int) else min(unit, NU - 1)
                    wait(pe, tp_hi, G * (made + 1))
                    wait(pe, tp_lo, G * (made + 1))
                else:
                    made = unit if not isinstance(unit, int) else min(unit, NU - 1)
                    wait(pe, u_out, 4 * (made + 1))
                if live(it, NTT):
                    logits(it, j)
                if live(it - 2, NTT):
                    dispatch(it - 2, j)
                state["lg"] = 4 * it + j + 1 if live(it, NTT) else 4 * NTT
                state["xt"] = 4 * (it - 2) + j + 1 if live(it - 2, NTT) else 0
                for part in range(2):
                    if live(v - 2, NV):
                        output(v - 2, (j + 2) % 4, unit - 1, part)
                    two = (2 * part, 2 * part + 1)
                    if j % 2 == 1 and live(unit + 1, NU):
                        make_tp(unit + 1, (j // 2 + 1) % 2, (2 * it + j // 2 + 1) // NPAIR, two)
                    if j % 2 == 0 and live(unit, NU):
                        make_u(unit, (j // 2) % 2, (2 * it + j // 2) // NPAIR, two)

            state["lg"] = state["xt"] = 0
            make_tp(0, 0, 0)
            run(pe, step)

        @block.scalar
        def _(act):
            def transposed_out(v, q):
                if live(v, NV):
                    for k in range(3):
                        act.wait_ge(t_mm, 3 * v + k + 1)
                        wait(act, av_mm, v)
                        nc.scalar.activation(pT[:, k, :], ps_t[:, (q + k) % 2, :], ACT.Copy).then_inc(t_out, 1)

            def softmax_exp(v, j):
                q = j % 2
                wait(act, t_mm, 3 * (v - 1))
                for k in range(3):
                    act.wait_ge(max_done, 3 * v + k + 1)
                    if k == 0:
                        wait(act, inv_done, v - 1)
                    for i in range(G if k == 0 else 2):
                        h = i if k == 0 else 2 * (k - 1) + i
                        c = h if k == 0 else G + h
                        width = P if k == 0 else S
                        dst = e0[q][:, h, :] if k == 0 else e1[q][:, h, :]
                        ins = nc.scalar.activation(dst, ps_s[:, k, i * width:(i + 1) * width], ACT.Exp,
                                                   bias=neg_max[:, q, c:c + 1], accum_out=total[:, q, c:c + 1])
                    ins.then_inc(exp_done, 1)

            def step(it, j):
                v = 4 * it + j
                unit = 2 * it + j // 2
                transposed_out(v - 2, j % 2)
                if live(v, NV):
                    softmax_exp(v, j)
                if j % 2 == 0 and live(unit, NU):
                    wait(act, av_mm, 2 * (unit - 1))
                for part in range(2):
                    half = bass.ds(((it - 1) % 2) * NS_ + part * NS_ // 2, NS_ // 2)
                    if j == 1 and live(it - 1, NTT):
                        act.wait_ge(d_sub, it)
                        nc.scalar.activation(disp[:, half], disp[:, half], ACT.Exp).then_inc(d_exp, 1)
                    if j == 2 and live(it - 1, NTT):
                        act.wait_ge(c_sub, it)
                        nc.scalar.activation(logit[:, half], logit[:, half], ACT.Exp).then_inc(c_exp, 1)
                    two = (2 * part, 2 * part + 1)
                    if j % 2 == 1 and live(unit + 1, NU):
                        take_tp(unit + 1, two)
                    if j % 2 == 0 and live(unit, NU):
                        for i in two:
                            act.wait_ge(u_mm, 4 * unit + i + 1)
                            nc.scalar.activation(u[(j // 2) % 2][:, i, :], ps_tu[:, i % 2, :],
                                                 ACT.Copy).then_inc(u_out, 1)

            def take_tp(unit, jobs=range(G)):
                wait(act, s_mm, 6 * unit)
                for i in jobs:
                    act.wait_ge(tp_mm, G * unit + i + 1)
                    nc.scalar.activation(tp[0][:, i, :], ps_tu[:, i % 2, :], ACT.Copy).then_inc(tp_hi, 1)

            take_tp(0)
            run(act, step)

        @block.vector
        def _(dve):
            def bank_max(v, j):
                q = j % 2
                for k in range(3):
                    dve.wait_ge(s_mm, 3 * v + k + 1)
                    if k == 0:
                        wait(dve, exp_done, 3 * (v - 1))
                    heads = G if k == 0 else 2
                    c = 0 if k == 0 else G + 2 * (k - 1)
                    nc.vector.tensor_reduce(neg_max[:, q, c:c + heads],
                                            ps_s[:, k, :].rearrange("p (h t) -> p h t", h=heads),
                                            AX.X, ALU.max, negate=True).then_inc(max_done, 1)

            def take_tp_lo(unit):
                for i in range(G):
                    dve.wait_ge(tp_hi, G * unit + i + 1)
                    nc.vector.tensor_tensor(tp[1][:, i, :], ps_tu[:, i % 2, :], f32(tp[0][:, i, :]),
                                            ALU.subtract).then_inc(tp_lo, 1)

            def step(it, j):
                v = 4 * it + j
                unit = 2 * it + j // 2
                t = it - 1
                if j % 2 == 0 and live(unit - 2, NU):
                    dve.wait_ge(av_mm, 2 * (unit - 1))
                    wait(dve, o_out, unit - 2)
                    o = o_acc[:, bass.ds(((unit - 2) % NPAIR) * PT, PT)]
                    nc.vector.tensor_tensor(o, ps_o[:, 0, :], o, ALU.add).then_inc(o_out, 1)
                if live(v, NV):
                    bank_max(v, j)
                if live(it, NTT):
                    if isinstance(it, int) and it == 0 and j == 0:
                        dve.wait_ge(bias_in, 16)
                    dve.wait_ge(lg_mm, 4 * it + j + 1)
                    if j == 0:
                        wait(dve, c_sum, it - 1)
                    nc.vector.tensor_tensor(logit[:, bass.ds((it % 2) * NS_ + j * BK, BK)], ps_tu[:, 0, :],
                                            bias[:, j * BK:(j + 1) * BK], ALU.add).then_inc(lg_out, 1)
                if live(it - 2, NTT):
                    dve.wait_ge(xt_mm, 4 * (it - 2) + j + 1)
                    wait(dve, xt_out, 4 * (it - 3) + j + 1)
                    acc = xt_acc[:, j * BK:(j + 1) * BK]
                    nc.vector.tensor_tensor(acc, ps_tu[:, 1, :], acc, ALU.add).then_inc(xt_out, 1)
                if live(v, NV):
                    dve.wait_ge(exp_done, 3 * v + 3)
                    wait(dve, norm_done, v - 1)
                    nc.vector.reciprocal(inv[:, j % 2, :], total[:, j % 2, :]).then_inc(inv_done, 1)
                if j % 2 == 1 and live(unit + 1, NU):
                    take_tp_lo(unit + 1)
                if live(t, NTT):
                    lt = logit[:, bass.ds((t % 2) * NS_, NS_)]
                    dt = disp[:, bass.ds((t % 2) * NS_, NS_)]
                    lt_e = lt.rearrange("p (e s) -> p e s", s=NP_)
                    dt_e = dt.rearrange("p (e s) -> p e s", s=NP_)
                    if j == 0:
                        dve.wait_ge(lg_out, 4 * t + 4)
                        wait(dve, d_sub, t)
                        nc.vector.tensor_reduce(gmax[:], lt_e, AX.X, ALU.max).then_inc(g_done, 1)
                        dve.wait_ge(g_done, t + 1)
                        wait(dve, xt_mm, 4 * (t - 1))
                        nc.vector.tensor_tensor(dt_e, lt_e, gmax[:].unsqueeze(2).to_broadcast([P, NE, NP_]),
                                                ALU.subtract).then_inc(d_sub, 1)
                    if j == 1:
                        nc.vector.tensor_reduce(m_all[:, bass.ds(t * NP_, NP_)],
                                                lt.rearrange("p (e s) -> p s e", s=NP_), AX.X,
                                                ALU.max).then_inc(m_done, 1)
                    if j == 2:
                        dve.wait_ge(d_exp, 2 * (t + 1))
                        nc.vector.memset(spare[:], 0.0)
                        nc.vector.tensor_reduce(dsum[:], dt_e, AX.X, ALU.add).then_inc(d_sum, 1)
                        dve.wait_ge(d_sum, t + 1)
                        wait(dve, d_norm, t)
                        nc.vector.reciprocal(dinv[:], dsum[:]).then_inc(d_inv, 1)
                    if j == 3:
                        dve.wait_ge(c_exp, 2 * (t + 1))
                        nc.vector.tensor_reduce(c_all[:, bass.ds(t * NP_, NP_)],
                                                lt.rearrange("p (e s) -> p s e", s=NP_), AX.X,
                                                ALU.add).then_inc(c_sum, 1)

            take_tp_lo(0)
            run(dve, step)

        @block.gpsimd
        def _(pool):
            def step(it, j):
                v = 4 * it + j
                t = it - 1
                if j == 2 and live(t, NTT):
                    pool.wait_ge(m_done, t + 1)
                    lt = logit[:, bass.ds((t % 2) * NS_, NS_)].rearrange("p (e s) -> p e s", s=NP_)
                    nc.gpsimd.tensor_tensor(lt, lt, m_all[:, bass.ds(t * NP_, NP_)].unsqueeze(1)
                                            .to_broadcast([P, NE, NP_]), ALU.subtract).then_inc(c_sub, 1)
                if j == 3 and live(t, NTT):
                    pool.wait_ge(d_inv, t + 1)
                    dt = disp[:, bass.ds((t % 2) * NS_, NS_)].rearrange("p (e s) -> p e s", s=NP_)
                    nc.gpsimd.tensor_tensor(dt, dt, dinv[:].unsqueeze(2).to_broadcast([P, NE, NP_]),
                                            ALU.mult).then_inc(d_norm, 1)
                if live(v, NV):
                    q = j % 2
                    pool.wait_ge(inv_done, v + 1)
                    nc.gpsimd.tensor_tensor(e0[q][:], e0[q][:], inv[:, q, 0:G].unsqueeze(2)
                                            .to_broadcast([P, G, P]), ALU.mult)
                    nc.gpsimd.tensor_tensor(e1[q][:], e1[q][:], inv[:, q, G:2 * G].unsqueeze(2)
                                            .to_broadcast([P, G, S]), ALU.mult).then_inc(norm_done, 1)

            run(pool, step)


def experts_phase(nc, env):
    with ExitStack() as ctx:
        def sb(name, shape, dt=F32):
            return ctx.enter_context(nc.sbuf_tensor(name, shape, dt))

        def sem(name):
            return ctx.enter_context(nc.semaphore(name))

        ew = sb("ew", [P, NE, D])
        eb = sb("eb", [P, NST, D])
        xslot = sb("xslot", [P, NST, D])
        xhT = sb("xhT", [P, NS_])
        stats = sb("stats2", [P, NST, 6])
        mv = sb("mv2", [P, NST, 2])
        var, root, quot, rstd = (sb(n, [P, NST]) for n in ("var2", "root2", "quot2", "rstd2"))
        ln_c = sb("ln_c", [P, NTT * NP_])
        lse_parts = sb("lse_parts", [P, NTT, 2, NP_], F32R)
        ps = ctx.enter_context(nc.psum_tensor("ps_e", [P, 8, BK], F32))

        ew_in, eb_in = sem("ew_in"), sem("eb_in")
        clip_done, xs_mm, xs_out, ln2, root_done, xhat, th = (
            sem(n) for n in ("clip_done", "xs_mm", "xs_out", "ln2", "root_done", "xhat", "th"))
        xh_mm, xh_out, y_mm, y_out = (sem(n) for n in ("xh_mm", "xh_out", "y_mm", "y_out"))
        lnc_done, lse_done, lse_split, lt_mm, lt_out = (
            sem(n) for n in ("lnc_done", "lse_done", "lse_split", "lt_mm", "lt_out"))
        ident, xt_acc, m_all, c_all = env["ident"], env["xt_acc"], env["m_all"], env["c_all"]
        y_t, lseT = env["y_t"], env["lseT"]
        NQ = NST // 4
        NL = NTT // 4

        block = ctx.enter_context(nc.Block())

        @block.sync
        def _(sp):
            sp.dma_start(ew[:], env["expert_w"].rearrange("n d h -> d n h")).then_inc(ew_in, 16)
            per_tile = env["expert_b"].rearrange("(t r) h -> r t h", r=4)
            for r in range(4):
                sp.dma_start(eb[NP_ * r:NP_ * (r + 1)], per_tile[r].partition_broadcast(NP_)).then_inc(eb_in, 16)
            sp.wait_ge(ew_in, 16)
            sp.wait_ge(eb_in, 64)

        @block.scalar
        def _(act):
            nc.scalar.activation(ln_c[:], c_all[:], ACT.Ln).then_inc(lnc_done, 1)
            for c in range(NQ):
                act.wait_ge(xs_mm, c + 1)
                nc.scalar.activation(xslot[:, 4 * c:4 * c + 4, :], ps[:, c, :], ACT.Copy).then_inc(xs_out, 1)
            act.wait_ge(ln2, 1)
            nc.scalar.activation(root[:], var[:], ACT.Sqrt).then_inc(root_done, 1)
            for c in range(NL):
                act.wait_ge(lt_mm, c + 1)
                nc.scalar.activation(lseT[:, c * BK:(c + 1) * BK], ps[0:2 * NP_, 4 + c % 4, :],
                                     ACT.Copy).then_inc(lt_out, 1)
            for c in range(NQ):
                act.wait_ge(xhat, c + 1)
                part = xslot[:, 4 * c:4 * c + 4, :]
                nc.scalar.activation(part, part, ACT.Tanh).then_inc(th, 1)
            for c in range(NQ):
                act.wait_ge(xh_mm, c + 1)
                nc.scalar.activation(xhT[:, c * BK:(c + 1) * BK], ps[:, c, :], ACT.Copy).then_inc(xh_out, 1)

        @block.vector
        def _(dve):
            nc.vector.tensor_scalar(xt_acc[:], xt_acc[:], -33000.0, 65000.0, ALU.max, ALU.min).then_inc(clip_done, 1)
            dve.wait_ge(lnc_done, 1)
            nc.vector.tensor_tensor(ln_c[:], ln_c[:], m_all[:], ALU.add).then_inc(lse_done, 1)
            dve.wait_ge(lse_done, 1)
            by_tile = ln_c[:].rearrange("p (t s) -> p t s", s=NP_)
            nc.vector.tensor_copy(lse_parts[:, :, 0, :], by_tile).then_inc(lse_split, 1)
            dve.wait_ge(lse_split, 1)
            nc.vector.tensor_tensor(lse_parts[:, :, 1, :], by_tile, f32(lse_parts[:, :, 0, :]),
                                    ALU.subtract).then_inc(lse_split, 1)
            for t in range(NST):
                if t % 4 == 0:
                    dve.wait_ge(xs_out, t // 4 + 1)
                nc.vector.bn_stats(stats[:, t, :], xslot[:, t, :])
            dve.drain()
            for t in range(NST):
                nc.vector.bn_aggr(mv[:, t, :], stats[:, t, :])
            dve.drain()
            nc.vector.tensor_scalar(var[:], mv[:, :, 1], EPS, None, ALU.add).then_inc(ln2, 1)
            dve.wait_ge(root_done, 1)
            nc.vector.reciprocal(quot[:], root[:]).then_inc(ln2, 1)
            dve.wait_ge(ln2, 2)
            nc.vector.tensor_tensor(quot[:], quot[:], var[:], ALU.mult).then_inc(ln2, 1)
            dve.wait_ge(ln2, 3)
            nc.vector.tensor_tensor(quot[:], quot[:], root[:], ALU.add).then_inc(ln2, 1)
            dve.wait_ge(ln2, 4)
            nc.vector.tensor_scalar(quot[:], quot[:], 0.5, None, ALU.mult).then_inc(ln2, 1)
            dve.wait_ge(ln2, 5)
            nc.vector.reciprocal(rstd[:], quot[:]).then_inc(ln2, 1)
            dve.wait_ge(ln2, 6)
            for t in range(NST):
                ins = nc.vector.tensor_scalar(xslot[:, t, :], xslot[:, t, :], mv[:, t, 0:1], rstd[:, t:t + 1],
                                              ALU.subtract, ALU.mult)
                if t % 4 == 3:
                    ins.then_inc(xhat, 1)
            dve.wait_ge(eb_in, 64)
            for c in range(NQ):
                dve.wait_ge(y_mm, c + 1)
                part = slice(4 * c, 4 * c + 4)
                nc.vector.tensor_tensor(eb[:, part, :], ps[:, 4 + c, :].rearrange("p (t h) -> p t h", t=4),
                                        eb[:, part, :], ALU.add).then_inc(y_out, 1)
                dve.wait_ge(y_out, 3 * c + 1)
                nc.vector.tensor_copy(y_t[0][:, part, :], eb[:, part, :]).then_inc(y_out, 1)
                dve.wait_ge(y_out, 3 * c + 2)
                nc.vector.tensor_tensor(y_t[1][:, part, :], eb[:, part, :], f32(y_t[0][:, part, :]),
                                        ALU.subtract).then_inc(y_out, 1)

        @block.tensor
        def _(pe):
            pe.wait_ge(clip_done, 1)
            for t in range(NST):
                mm = pe.transpose(ps[:, t // 4, (t % 4) * P:(t % 4 + 1) * P], xt_acc[:, t * P:(t + 1) * P], ident[:])
                if t % 4 == 3:
                    mm.then_inc(xs_mm, 1)
            pe.wait_ge(lse_split, 2)
            for t in range(NTT):
                if t % 4 == 0 and t >= 16:
                    pe.wait_ge(lt_out, t // 4 - 3)
                mm = pe.transpose(ps[0:2 * NP_, 4 + (t // 4) % 4, (t % 4) * P:(t % 4 + 1) * P],
                                  f32(lse_parts[:, t, :, :].rearrange("p a b -> p (a b)")), ident[:])
                if t % 4 == 3:
                    mm.then_inc(lt_mm, 1)
            for t in range(NST):
                if t % 4 == 0:
                    pe.wait_ge(th, t // 4 + 1)
                mm = pe.transpose(ps[:, t // 4, (t % 4) * P:(t % 4 + 1) * P], xslot[:, t, :], ident[:])
                if t % 4 == 3:
                    mm.then_inc(xh_mm, 1)
            pe.wait_ge(ew_in, 16)
            pe.wait_ge(lt_out, NL)
            for t in range(NST):
                if t % 4 == 0:
                    pe.wait_ge(xh_out, t // 4 + 1)
                for r in range(4):
                    mm = pe.matmul(ps[NP_ * r:NP_ * (r + 1), 4 + t // 4, (t % 4) * P:(t % 4 + 1) * P],
                                   xhT[:, t * P + NP_ * r:t * P + NP_ * (r + 1)], ew[:, 4 * t + r, :],
                                   start=True, stop=True, skip_group_check=True)
                if t % 4 == 3:
                    mm.then_inc(y_mm, 1)


def combine_phase(nc, env):
    with ExitStack() as ctx:
        def sb(name, shape, dt=F32):
            return ctx.enter_context(nc.sbuf_tensor(name, shape, dt))

        def psum(name, banks):
            return ctx.enter_context(nc.psum_tensor(name, [P, banks, BK], F32))

        def sem(name):
            return ctx.enter_context(nc.semaphore(name))

        R = 4
        LAG = 2
        cT = sb("cT", [P, R, BK])
        c_hi, c_lo = (sb(n, [P, R, BK], F32R) for n in ("c_hi", "c_lo"))
        fin = sb("fin", [P, PT])
        xres = sb("xres", [P, 2, 4, D])
        res = sb("res", [P, 2, 4, D])
        ps_l, ps_y, ps_f = psum("ps_l", R), psum("ps_y", 2), psum("ps_f", 1)
        lt_mm, c_exp, c_low, y_mm, fin_done, f_mm, res_done = (
            sem(n) for n in ("lt2_mm", "c2_exp", "c2_low", "y2_mm", "fin_done", "f_mm", "res_done"))
        x_in = [sem("x_in0"), sem("x_in1")]
        stored = [sem("stored0"), sem("stored1")]
        ident, xT, phiT, nsel, lseT = env["ident"], env["xT"], env["phiT"], env["nsel"], env["lseT"]
        y_t, phibT, o_acc = env["y_t"], env["phibT"], env["o_acc"]
        x_pair = env["x"].rearrange("(n t p) d -> n p t d", p=P, t=4)
        out_pair = env["out"].rearrange("(n t p) d -> n p t d", p=P, t=4)

        block = ctx.enter_context(nc.Block())

        @block.sync
        def _(sp):
            for p in range(NPAIR):
                wait(sp, res_done, p - 1)
                sp.dma_start(xres[:, p % 2], x_pair[p]).then_inc(x_in[p % 2], 16)

        @block.gpsimd
        def _(pool):
            for p in range(NPAIR):
                pool.wait_ge(res_done, p + 1)
                pool.dma_start(out_pair[p], res[:, p % 2]).then_inc(stored[p % 2], 16)
            for q in range(2):
                pool.wait_ge(stored[q], 16 * NPAIR // 2)

        @block.tensor
        def _(pe):
            def untranspose(p):
                pe.wait_ge(fin_done, p + 1)
                wait(pe, res_done, p)
                for i in range(4):
                    mm = pe.transpose(ps_f[:, 0, i * P:(i + 1) * P], fin[:, i * P:(i + 1) * P], ident[:])
                mm.then_inc(f_mm, 1)

            def logits_t(p, st):
                n = NST * p + st
                w, tok = slice(st * P, (st + 1) * P), bass.ds(p * PT, PT)
                wait(pe, c_exp, n - R + 1)
                product3(pe, ps_l[:, st % R, :], phiT[0][:, w], phiT[1][:, w], xT[0][:, tok], xT[1][:, tok],
                         stop=False)
                pe.matmul(ps_l[:, st % R, :], nsel[:], lseT[:, tok], start=False, stop=True,
                          skip_group_check=True).then_inc(lt_mm, 1)

            def mix(p, q, st):
                pe.wait_ge(c_low, NST * p + st + 1)
                if st == 0:
                    wait(pe, fin_done, p - 1)
                product3(pe, ps_y[:, q, :], y_t[0][:, st, :], y_t[1][:, st, :], c_hi[:, st % R, :],
                         c_lo[:, st % R, :], start=(st == 0), stop=(st == NST - 1)).then_inc(y_mm, 1)

            def pair(p, q):
                for st in range(NST):
                    logits_t(p, st)
                    if st >= LAG:
                        mix(p, q, st - LAG)
                    elif live(p - 1, NPAIR):
                        mix(p - 1, 1 - q, NST + st - LAG)
                    if st == 6 and live(p - 1, NPAIR):
                        untranspose(p - 1)

            pair(0, 0)
            pair(1, 1)
            with pe.Fori(1, NPAIR // 2) as pp:
                for q in range(2):
                    pair(2 * pp + q, q)
            for st in range(NST - LAG, NST):
                mix(NPAIR - 1, 1, st)
            untranspose(NPAIR - 1)

        @block.scalar
        def _(act):
            def pair(p):
                for st in range(NST):
                    act.wait_ge(lt_mm, NST * p + st + 1)
                    wait(act, y_mm, NST * p + st - R + 1)
                    nc.scalar.activation(c_hi[:, st % R, :], ps_l[:, st % R, :], ACT.Exp, bias=phibT[:, st:st + 1])
                    nc.scalar.activation(cT[:, st % R, :], ps_l[:, st % R, :], ACT.Exp,
                                         bias=phibT[:, st:st + 1]).then_inc(c_exp, 1)

            pair(0)
            with act.Fori(1, NPAIR) as p:
                pair(p)

        @block.vector
        def _(dve):
            def add_x(p):
                dve.wait_ge(f_mm, p + 1)
                dve.wait_ge(x_in[p % 2], 16 * (p // 2 + 1))
                wait(dve, stored[p % 2], 16 * (p // 2))
                nc.vector.tensor_tensor(res[:, p % 2], ps_f[:, 0, :].rearrange("p (t d) -> p t d", t=4),
                                        xres[:, p % 2], ALU.add).then_inc(res_done, 1)

            def low_parts(p, tiles):
                for st in tiles:
                    dve.wait_ge(c_exp, NST * p + st + 1)
                    wait(dve, y_mm, NST * p + st - R + 1)
                    nc.vector.tensor_tensor(c_lo[:, st % R, :], cT[:, st % R, :], f32(c_hi[:, st % R, :]),
                                            ALU.subtract).then_inc(c_low, 1)

            def finish(p):
                dve.wait_ge(y_mm, NST * (p + 1))
                wait(dve, f_mm, p)
                nc.vector.tensor_tensor(fin[:], ps_y[:, p % 2, :], o_acc[:, p * PT:(p + 1) * PT],
                                        ALU.add).then_inc(fin_done, 1)

            EARLY = 3
            for p in range(NPAIR + 1):
                if p < NPAIR:
                    low_parts(p, range(EARLY))
                if p > 0:
                    finish(p - 1)
                if p < NPAIR:
                    low_parts(p, range(EARLY, 8))
                if p > 0:
                    add_x(p - 1)
                if p < NPAIR:
                    low_parts(p, range(8, NST))


def build(nc, x, wq, wk, wv, wo, lq1, lk1, lq2, lk2, phi_w, phi_b, expert_w, expert_b, out):
    with ExitStack() as ctx:
        def sb(name, shape, dt=F32):
            return ctx.enter_context(nc.sbuf_tensor(name, shape, dt))

        env = dict(x=x.rearrange("b s d -> (b s) d"), wq=wq, wk=wk, wv=wv, wo=wo, lq1=lq1, lk1=lk1, lq2=lq2, lk2=lk2,
                   phi_w=phi_w, phi_b=phi_b, expert_w=expert_w, expert_b=expert_b,
                   out=out.rearrange("b s d -> (b s) d"))
        env["ab_dram"] = nc.dram_tensor("ab_scratch", [2, NG, 2, P, G * P], F32, kind="Internal").ap()
        env["xn_dram"] = nc.dram_tensor("xn_scratch", [NTT, P, D], F32, kind="Internal").ap()
        env["ident"] = sb("ident", [P, P])
        env["identb"] = sb("identb", [P, P], BF16)
        env["mask"] = sb("mask", [P, G, P], BF16)
        env["xT"] = [sb(f"xT{h}", [P, NT], F32R) for h in range(2)]
        env["phiT"] = [sb(f"phiT{h}", [P, NS_], F32R) for h in range(2)]
        env["phibT"] = sb("phibT", [P, NST])
        env["nsel_f"] = sb("nsel_f", [2 * NP_, P])
        env["nsel"] = sb("nsel", [2 * NP_, P], F32R)
        env["o_acc"] = sb("o_acc", [P, NT])
        env["xt_acc"] = sb("xt_acc", [P, NS_])
        env["m_all"] = sb("m_all", [P, NTT * NP_])
        env["c_all"] = sb("c_all", [P, NTT * NP_])
        setup_phase(nc, env)
        main_phase(nc, env)
        env["y_t"] = [sb(f"y_t{h}", [P, NST, D], F32R) for h in range(2)]
        env["lseT"] = sb("lseT", [2 * NP_, NT], F32R)
        experts_phase(nc, env)
        combine_phase(nc, env)


_INS = ["L0_attn_x", "L0_attn_Wq", "L0_attn_Wk", "L0_attn_Wv", "L0_attn_Wo", "L0_attn_lq1", "L0_attn_lk1",
        "L0_attn_lq2", "L0_attn_lk2", "L0_ffn_phi_w", "L0_ffn_phi_b", "L0_ffn_expert_w", "L0_ffn_expert_b"]


def kernel(**inputs):
    import concourse.bacc as bacc
    from concourse.bass_utils import run_bass_kernel_spmd as run

    nc = bacc.Bacc("TRN2", target_bir_lowering=False, num_devices=1)
    arrays, args = {}, []
    for name in _INS:
        a = np.ascontiguousarray(inputs[name])
        arrays[f"in_{name}"] = a
        args.append(nc.dram_tensor(f"in_{name}", a.shape, mybir.dt.from_np(a.dtype), kind="ExternalInput").ap())
    out = nc.dram_tensor("out_dram", (NB, S, D), F32, kind="ExternalOutput").ap()
    build(nc, *args, out)
    r = run(nc, [arrays], core_ids=[0])
    return r.results[0]["out_dram"]
```

```python
from contextlib import ExitStack

import numpy as np

import concourse.bass as bass
from concourse import mybir
from concourse.alu_op_type import AluOpType as ALU

F32 = mybir.dt.float32
F32R = mybir.dt.float32r
BF16 = mybir.dt.bfloat16
ACT = mybir.ActivationFunctionType
AX = mybir.AxisListType

P = 128
NB, S, D = 16, 256, 128
NT = NB * S
NTT = NT // P
DH = 64
NH = 16
NHH = 2 * NH
G = 4
NG = NHH // G
GV = G * DH
NPAIR = NB // 2
PT = 2 * S
NU = NG * NPAIR
NV = 2 * NU
NE, NP_, NS_ = 64, 32, 2048
NST = NS_ // P
BK = 512
EB = BK // NP_
LAMBDA_INIT = 0.8
OUT_SCALE = 1.0 - LAMBDA_INIT
SCORE_SCALE = DH ** -0.5
EPS = 1e-5
MASKED = -1e30
ITER = NTT


def wait(eng, sem, value):
    if isinstance(value, int) and value <= 0:
        return
    eng.wait_ge(sem, value)


def head_half(g, i):
    return NH * (i // 2) + 4 * (g // 2) + 2 * (i % 2) + g % 2


def live(i, n):
    return not isinstance(i, int) or 0 <= i < n


def f32(ap):
    return ap.bitcast(F32)


def product3(pe, out, w_hi, w_lo, m_hi, m_lo, start=True, stop=True):
    pe.matmul(out, w_hi, m_hi, start=start, stop=False, skip_group_check=True)
    pe.matmul(out, w_hi, m_lo, start=False, stop=False, skip_group_check=True)
    return pe.matmul(out, w_lo, m_hi, start=False, stop=stop, skip_group_check=True)


def setup_phase(nc, env):
    NBANK = 6
    with ExitStack() as ctx:
        def sb(name, shape, dt=F32):
            return ctx.enter_context(nc.sbuf_tensor(name, shape, dt))

        def sem(name):
            return ctx.enter_context(nc.semaphore(name))

        x_sb = sb("x_sb", [P, NTT, D])
        wq, wk, wv = (sb(n, [P, NHH * DH]) for n in ("wq", "wk", "wv"))
        wo = sb("wo", [P, NG, D])
        v_parts = [sb(f"v_part{h}", [P, NG * GV], F32R) for h in range(2)]
        wo_parts = [sb(f"wo_part{h}", [P, NG, D], F32R) for h in range(2)]
        phi_w = sb("phi_w", [P, NST, D])
        wT = {n: sb(n + "T", [P, NHH * DH]) for n in ("wq", "wk")}
        stage = sb("stage", [P, 4, 2, BK], F32R)
        lqk = sb("lqk", [P, 4, DH])
        lprod = sb("lprod", [P, 2, DH])
        ldot = sb("ldot", [P, 2])
        lexp = sb("lexp", [P, 2])
        lam = sb("lam", [P, 1])
        neg_lam = sb("neg_lam", [P, 1])
        stats = sb("stats", [P, NTT, 6])
        mv = sb("mv", [P, NTT, 2])
        var = sb("var", [P, NTT])
        root = sb("root", [P, NTT])
        rstd = sb("rstd", [P, NTT])
        quot = sb("quot", [P, NTT])
        phib_rows = sb("phib_rows", [NST, P])
        ps = ctx.enter_context(nc.psum_tensor("ps_setup", [P, NBANK, BK], F32))
        ps_b = ctx.enter_context(nc.psum_tensor("ps_phib", [P, BK], F32))

        loaded = {n: sem("loaded_" + n) for n in ("x", "phi", "wq", "wk", "wv", "wo", "l", "phib")}
        s_const = sem("s_const")
        job_done = sem("job_done")
        hi_out = sem("hi_out")
        lo_out = sem("lo_out")
        ln_step = sem("ln_step")
        var_root = sem("var_root")
        xn_ready = sem("xn_ready")
        lam_step = sem("lam_step")
        lam_exp = sem("lam_exp")
        w_hi, w_lo = sem("w_hi"), sem("w_lo")
        a_stored = [sem(f"a_stored{i}") for i in range(4)]
        w_stored = sem("w_stored")
        xn_stored = sem("xn_stored")
        phib_done = sem("phib_done")
        phib_out = sem("phib_out")

        ident, identb, mask = env["ident"], env["identb"], env["mask"]
        xT, phiT = env["xT"], env["phiT"]
        a_dram, v_dram, wo_dram, xn_dram = env["a_dram"], env["v_dram"], env["wo_dram"], env["xn_dram"]

        jobs = [("phi", i) for i in range(4)] + [("x", i) for i in range(8)]
        jobs += [("wq", i) for i in range(4)] + [("wk", i) for i in range(4)] + [("A", i) for i in range(NG)]
        SPLIT = ("phi", "x", "A")
        lo_count = [sum(k in SPLIT for k, _ in jobs[:n + 1]) for n in range(len(jobs))]
        at = {job: n for n, job in enumerate(jobs)}

        def parts(kind, i):
            if kind == "phi":
                return [t[:, i * BK:(i + 1) * BK] for t in phiT]
            if kind == "x":
                return [t[:, i * BK:(i + 1) * BK] for t in xT]
            return [stage[:, i % 4, h, :] for h in range(2)]

        def wv_quarters():
            for half in range(2):
                for r in range(2):
                    src = wv[:].rearrange("p (s k h r d) -> p s r k h d", s=2, h=2, r=2, d=DH)[:, half, r]
                    dst = [v[:].rearrange("p (k r s h d) -> p s r k h d", r=2, s=2, h=2, d=DH)[:, half, r]
                           for v in v_parts]
                    yield (OUT_SCALE if half == 0 else neg_lam[:]), src, dst

        block = ctx.enter_context(nc.Block())

        @block.sync
        def _(sp):
            sp.dma_start(x_sb[:], env["x"].rearrange("(t p) d -> p t d", p=P)).then_inc(loaded["x"], 16)
            sp.dma_start(phi_w[:], env["phi_w"].rearrange("(t p) d -> p t d", p=P)).then_inc(loaded["phi"], 16)
            for i, v in enumerate(("lq1", "lk1", "lq2", "lk2")):
                sp.dma_start(lqk[:, i, :], env[v].partition_broadcast(P)).then_inc(loaded["l"], 16)
            sp.dma_start(wv[:], env["wv"]).then_inc(loaded["wv"], 16)
            for h in range(2):
                for r in range(2):
                    sp.dma_start(wo[h * DH:(h + 1) * DH, r::2, :],
                                 env["wo"].rearrange("(k h r d) m -> h r d k m", h=2, r=2, d=DH)[h, r]
                                 ).then_inc(loaded["wo"], 16)
            sp.wait_ge(xn_ready, 1)
            sp.dma_start(xn_dram.rearrange("t p d -> p t d"), x_sb[:]).then_inc(xn_stored, 16)
            for i in range(NG):
                sp.wait_ge(hi_out, at[("A", i)] + 1)
                sp.wait_ge(lo_out, lo_count[at[("A", i)]])
                sp.dma_start(a_dram[i].rearrange("h p n -> p h n"), f32(stage[:, i % 4])).then_inc(a_stored[i % 4], 16)
            sp.wait_ge(w_hi, 5)
            sp.wait_ge(w_lo, 5)
            for h in range(2):
                sp.dma_start(v_dram[:, h].rearrange("g p n -> p g n"),
                             f32(v_parts[h][:]).rearrange("p (g n) -> p g n", g=NG)).then_inc(w_stored, 16)
                sp.dma_start(wo_dram[:, h].rearrange("g p n -> p g n"), f32(wo_parts[h][:])).then_inc(w_stored, 16)
            for q in range(4):
                sp.wait_ge(a_stored[q], 16 * NG // 4)
            sp.wait_ge(w_stored, 64)
            sp.wait_ge(xn_stored, 16)

        @block.gpsimd
        def _(pool):
            for t in (ident, identb):
                nc.gpsimd.memset(t[:], 0.0).then_inc(s_const, 1)
            nc.gpsimd.memset(mask[:], 0.0).then_inc(s_const, 1)
            pool.wait_ge(s_const, 3)
            for t in (ident, identb):
                nc.gpsimd.affine_select(out=t[:], in_=t[:], compare_op=ALU.not_equal, fill=1.0, base=0,
                                        pattern=[[-1, P]], channel_multiplier=1).then_inc(s_const, 1)
            nc.gpsimd.affine_select(out=mask[:], in_=mask[:], compare_op=ALU.is_ge, fill=MASKED, base=0,
                                    pattern=[[0, G], [-1, P]], channel_multiplier=1).then_inc(s_const, 1)
            nc.gpsimd.memset(env["o_acc"][:], 0.0)
            nc.gpsimd.memset(env["xt_acc"][:], 0.0)
            nsel = env["nsel_f"]
            nc.gpsimd.memset(nsel[:], 0.0).then_inc(s_const, 1)
            pool.wait_ge(s_const, 7)
            for n, base in enumerate((0, -NP_)):
                nc.gpsimd.affine_select(out=nsel[:], in_=nsel[:], compare_op=ALU.not_equal, fill=-1.0, base=base,
                                        pattern=[[0, P // NP_], [-1, NP_]], channel_multiplier=1).then_inc(s_const, 1)
                pool.wait_ge(s_const, 8 + n)

        @block.scalar
        def _(act):
            act.dma_start(wq[:], env["wq"]).then_inc(loaded["wq"], 16)
            act.dma_start(wk[:], env["wk"]).then_inc(loaded["wk"], 16)
            act.dma_start(phib_rows[:], env["phi_b"].rearrange("(t p) -> t p", p=P)).then_inc(loaded["phib"], 16)
            act.wait_ge(ln_step, 1)
            nc.scalar.activation(root[:], var[:], ACT.Sqrt).then_inc(var_root, 1)
            act.wait_ge(lam_step, 2)
            nc.scalar.activation(lexp[:], ldot[:], ACT.Exp).then_inc(lam_exp, 1)
            act.wait_ge(phib_done, 1)
            nc.scalar.activation(env["phibT"][:], ps_b[:, 0:NST], ACT.Copy).then_inc(phib_out, 1)
            for n, (kind, i) in enumerate(jobs):
                bank = ps[:, n % NBANK, :]
                act.wait_ge(job_done, n + 1)
                if kind in SPLIT:
                    if kind == "A" and i >= 4:
                        act.wait_ge(a_stored[i % 4], 16 * (i // 4))
                    hi = parts(kind, i)[0]
                    if kind == "A":
                        nc.scalar.activation(hi, bank, ACT.Copy, scale=SCORE_SCALE).then_inc(hi_out, 1)
                    else:
                        nc.scalar.activation(hi, bank, ACT.Copy).then_inc(hi_out, 1)
                else:
                    nc.scalar.activation(wT[kind][:, i * BK:(i + 1) * BK], bank, ACT.Copy).then_inc(hi_out, 1)
                if kind == "x" and i == 7:
                    act.wait_ge(loaded["wo"], 64)
                    nc.scalar.activation(wo_parts[0][:], wo[:], ACT.Copy).then_inc(w_hi, 1)
                    act.wait_ge(loaded["wv"], 16)
                    act.wait_ge(lam_step, 4)
                    for scale, src, dst in wv_quarters():
                        nc.scalar.activation(dst[0], src, ACT.Identity, scale=scale).then_inc(w_hi, 1)

        @block.vector
        def _(dve):
            dve.wait_ge(loaded["x"], 16)
            for t in range(NTT):
                nc.vector.bn_stats(stats[:, t, :], x_sb[:, t, :])
            dve.drain()
            for t in range(NTT):
                nc.vector.bn_aggr(mv[:, t, :], stats[:, t, :])
            dve.drain()
            nc.vector.tensor_scalar(var[:], mv[:, :, 1], EPS, None, ALU.add).then_inc(ln_step, 1)
            dve.wait_ge(var_root, 1)
            nc.vector.reciprocal(quot[:], root[:]).then_inc(ln_step, 1)
            dve.wait_ge(ln_step, 2)
            nc.vector.tensor_tensor(quot[:], quot[:], var[:], ALU.mult).then_inc(ln_step, 1)
            dve.wait_ge(ln_step, 3)
            nc.vector.tensor_tensor(quot[:], quot[:], root[:], ALU.add).then_inc(ln_step, 1)
            dve.wait_ge(ln_step, 4)
            nc.vector.tensor_scalar(quot[:], quot[:], 0.5, None, ALU.mult).then_inc(ln_step, 1)
            dve.wait_ge(ln_step, 5)
            nc.vector.reciprocal(rstd[:], quot[:]).then_inc(ln_step, 1)
            dve.wait_ge(ln_step, 6)
            for t in range(NTT):
                last = nc.vector.tensor_scalar(x_sb[:, t, :], x_sb[:, t, :], mv[:, t, 0:1], rstd[:, t:t + 1],
                                               ALU.subtract, ALU.mult)
            last.then_inc(xn_ready, 1)
            dve.wait_ge(loaded["l"], 64)
            nc.vector.tensor_tensor(lprod[:], lqk[:, 0:4:2, :], lqk[:, 1:4:2, :], ALU.mult).then_inc(lam_step, 1)
            dve.wait_ge(lam_step, 1)
            nc.vector.tensor_reduce(ldot[:], lprod[:], AX.X, ALU.add).then_inc(lam_step, 1)
            dve.wait_ge(lam_exp, 1)
            nc.vector.tensor_tensor(lam[:], lexp[:, 0:1], lexp[:, 1:2], ALU.subtract).then_inc(lam_step, 1)
            dve.wait_ge(lam_step, 3)
            nc.vector.tensor_scalar(neg_lam[:], lam[:], LAMBDA_INIT, -OUT_SCALE, ALU.add, ALU.mult).then_inc(lam_step, 1)
            dve.wait_ge(lam_step, 4)
            dve.wait_ge(s_const, 9)
            nc.vector.tensor_copy(env["nsel"][:], env["nsel_f"][:])
            for n, (kind, i) in enumerate(jobs):
                if kind not in SPLIT:
                    continue
                hi, lo = parts(kind, i)
                scale = SCORE_SCALE if kind == "A" else 1.0
                dve.wait_ge(hi_out, n + 1)
                nc.vector.scalar_tensor_tensor(out=lo, in0=ps[:, n % NBANK, :], scalar=scale, in1=f32(hi),
                                               op0=ALU.mult, op1=ALU.subtract).then_inc(lo_out, 1)
                if kind == "x" and i == 7:
                    dve.wait_ge(w_hi, 1)
                    nc.vector.tensor_tensor(wo_parts[1][:], wo[:], f32(wo_parts[0][:]), ALU.subtract).then_inc(w_lo, 1)
                    for n_hi, (scale, src, dst) in enumerate(wv_quarters()):
                        dve.wait_ge(w_hi, n_hi + 2)
                        nc.vector.scalar_tensor_tensor(out=dst[1], in0=src, scalar=scale, in1=f32(dst[0]),
                                                       op0=ALU.mult, op1=ALU.subtract).then_inc(w_lo, 1)

        @block.tensor
        def _(pe):
            pe.wait_ge(s_const, 6)
            pe.wait_ge(loaded["phib"], 16)
            pe.transpose(ps_b[:, 0:NST], phib_rows[:], ident[0:NST, 0:NST]).then_inc(phib_done, 1)
            need = {"phi": "phi", "wq": "wq", "wk": "wk"}
            for n, (kind, i) in enumerate(jobs):
                if n >= NBANK:
                    pe.wait_ge(hi_out, n - NBANK + 1)
                    wait(pe, lo_out, lo_count[n - NBANK])
                if kind in need and i == 0:
                    pe.wait_ge(loaded[need[kind]], 16)
                if kind == "x" and i == 0:
                    pe.wait_ge(xn_ready, 1)
                if kind == "A" and i == 0:
                    pe.wait_ge(hi_out, at[("wk", 3)] + 1)
                for j in range(4):
                    out = ps[:, n % NBANK, j * P:(j + 1) * P]
                    c = 4 * i + j
                    if kind == "phi":
                        mm = pe.transpose(out, phi_w[:, c, :], ident[:])
                    elif kind == "x":
                        mm = pe.transpose(out, x_sb[:, c, :], ident[:])
                    elif kind in wT:
                        src = {"wq": wq, "wk": wk}[kind]
                        mm = pe.transpose(out, src[:, c * P:(c + 1) * P], ident[:])
                    else:
                        c = head_half(i, j)
                        r0, t0 = (c % 2) * DH, (c // 2) * P
                        rows = slice(r0, r0 + DH)
                        mm = pe.matmul(out, wT["wk"][rows, t0:t0 + P], wT["wq"][rows, t0:t0 + P],
                                       start=True, stop=True, skip_group_check=True)
                mm.then_inc(job_done, 1)


def main_phase(nc, env):
    with ExitStack() as ctx:
        def sb(name, shape, dt=F32):
            return ctx.enter_context(nc.sbuf_tensor(name, shape, dt))

        def psum(name, banks):
            return ctx.enter_context(nc.psum_tensor(name, [P, banks, BK], F32))

        def sem(name):
            return ctx.enter_context(nc.semaphore(name))

        xs = [[sb(f"xs{q}{h}", [P, PT], F32R) for h in range(2)] for q in range(2)]
        a_w = [sb(f"a_w{h}", [P, G * P], F32R) for h in range(2)]
        v_w = [sb(f"v_w{h}", [P, GV], F32R) for h in range(2)]
        wo_w = [sb(f"wo_w{h}", [P, D], F32R) for h in range(2)]
        o_t = [sb(f"o_t{h}", [P, PT], F32R) for h in range(2)]
        tp = [sb(f"tp{h}", [P, G, PT], F32R) for h in range(2)]
        v_sb = [sb(f"v_sb{q}", [P, 4, GV]) for q in range(2)]
        e0 = [sb(f"e0{q}", [P, G, P]) for q in range(2)]
        e1 = [sb(f"e1{q}", [P, G, S]) for q in range(2)]
        pT = sb("pT", [P, 3, BK])
        neg_max = sb("neg_max", [P, 2, 2 * G])
        total = sb("total", [P, 2, 2 * G])
        inv = sb("inv", [P, 2, 2 * G])
        fx = [sb(f"fx{h}", [P, P], F32R) for h in range(2)]
        fxn = sb("fxn", [P, D])
        bias = sb("bias", [P, NS_])
        logit = sb("logit", [P, 2 * NS_])
        disp = sb("disp", [P, 2 * NS_])
        gmax = sb("gmax", [P, 4, EB])
        dsum = sb("dsum", [P, 4, EB])
        dinv = sb("dinv", [P, 4, EB])
        m_part = sb("m_part", [P, 4, NP_])
        c_part = sb("c_part", [P, 4, NP_])
        spare = sb("spare", [P, 20])
        pool_spare = sb("pool_spare", [P, 14])
        ps_tu, ps_s, ps_t, ps_o = psum("ps_tu", 2), psum("ps_s", 3), psum("ps_t", 2), psum("ps_o", 1)

        xs_in = [sem("xs_in0"), sem("xs_in1")]
        a_in, v_in, wo_in, fx_in, fxn_in, bias_in = (
            sem(n) for n in ("a_in", "v_in", "wo_in", "fx_in", "fxn_in", "bias_in"))
        tp_mm, v_mm, lg_mm, xt_mm, s_mm, t_mm, av_mm, wo_mm = (
            sem(n) for n in ("tp_mm", "v_mm", "lg_mm", "xt_mm", "s_mm", "t_mm", "av_mm", "wo_mm"))
        tp_hi, tp_lo, v_out, lg_out, xt_out, t_out, o_hi, o_lo, wo_out = (
            sem(n) for n in ("tp_hi", "tp_lo", "v_out", "lg_out", "xt_out", "t_out", "o_hi", "o_lo", "wo_out"))
        max_done, exp_done, inv_done, norm_done = (sem(n) for n in ("max_done", "exp_done", "inv_done", "norm_done"))
        g_done, d_sub, d_exp, d_sum, d_inv, d_norm = (
            sem(n) for n in ("g_done", "d_sub", "d_exp", "d_sum", "d_inv", "d_norm"))
        m_bank, m_done, c_sub, c_exp, c_bank, c_sum = (
            sem(n) for n in ("m_bank", "m_done", "c_sub", "c_exp", "c_bank", "c_sum"))

        def bank_of(buf, t, j):
            return buf[:, bass.ds((t % 2) * NS_ + j * BK, BK)]

        def by_expert(ap):
            return ap.rearrange("p (e s) -> p e s", s=NP_)

        def step_before(it, j):
            return (it, j - 1) if j > 0 else (it - 1, 3)

        ident, identb, mask = env["ident"], env["identb"], env["mask"]
        xT, phiT, o_acc, xt_acc = env["xT"], env["phiT"], env["o_acc"], env["xt_acc"]
        m_all, c_all = env["m_all"], env["c_all"]
        a_dram, v_dram, wo_dram, xn_dram = env["a_dram"], env["v_dram"], env["wo_dram"], env["xn_dram"]

        block = ctx.enter_context(nc.Block())

        def run(eng, step):
            for it in range(3):
                for j in range(4):
                    step(it, j)
            with eng.Fori(3, ITER - 1) as it:
                for j in range(4):
                    step(it, j)
            for it in range(ITER - 1, ITER + 1):
                for j in range(4):
                    step(it, j)

        @block.sync
        def _(sp):
            def load_xs(unit, q, pair):
                if not live(unit, NU):
                    return
                wait(sp, s_mm, 3 * (2 * (unit - 2) + 2))
                wait(sp, v_mm, 2 * (unit - 1))
                for h in range(2):
                    sp.dma_start(f32(xs[q][h][:]), f32(xT[h][:, bass.ds(pair * PT, PT)])).then_inc(xs_in[q], 16)

            def load_group(g, w, dram, count, per_unit, s_in):
                wait(sp, count, per_unit * NPAIR * g)
                for h in range(2):
                    sp.dma_start(f32(w[h][:]), dram[g, h]).then_inc(s_in, 16)

            def load_tile(t):
                if live(t, NTT):
                    wait(sp, lg_mm, 4 * t)
                    for h in range(2):
                        sp.dma_start(f32(fx[h][:]), f32(xT[h][:, bass.ds(t * P, P)])).then_inc(fx_in, 16)

            def load_tokens(t):
                if live(t, NTT):
                    wait(sp, xt_mm, 4 * t)
                    sp.dma_start(fxn[:], xn_dram[t]).then_inc(fxn_in, 16)

            def iteration(it, kk, g, last=False):
                load_xs(2 * it + 2, 0, (2 * kk + 2) % NPAIR)
                if kk == 0 and not (isinstance(g, int) and g == 0):
                    load_group(g, wo_w, wo_dram, wo_mm, 1, wo_in)
                if kk == per - 1 and not last:
                    load_group(g + 1, a_w, a_dram, tp_mm, G, a_in)
                    load_group(g + 1, v_w, v_dram, v_mm, 2, v_in)
                load_xs(2 * it + 3, 1, (2 * kk + 3) % NPAIR)
                load_tile(it + 1)
                load_tokens(it)

            per = NPAIR // 2
            load_group(0, a_w, a_dram, tp_mm, G, a_in)
            load_xs(0, 0, 0)
            load_group(0, v_w, v_dram, v_mm, 2, v_in)
            load_group(0, wo_w, wo_dram, wo_mm, 1, wo_in)
            load_xs(1, 1, 1)
            load_tile(0)
            sp.dma_start(bias[:], env["phi_b"].partition_broadcast(P)).then_inc(bias_in, 16)
            for it in range(per):
                iteration(it, it, 0)
            with sp.Fori(1, NG - 1) as g:
                for kk in range(per):
                    iteration(g * per + kk, kk, g)
            for kk in range(per):
                iteration(ITER - per + kk, kk, NG - 1, last=True)

        @block.tensor
        def _(pe):
            def transposes(v, q, ks):
                if ks[0] == 0:
                    pe.wait_ge(norm_done, v + 1)
                for k in ks:
                    n = 3 * v + k
                    bank = ps_t[:, (q + k) % 2, :]
                    wait(pe, t_out, n - 1)
                    for i in range(4):
                        if k == 2:
                            src = e1[q][:, i, P:S]
                        elif i % 2 == 0:
                            src = e0[q][:, 2 * k + i // 2, :]
                        else:
                            src = e1[q][:, 2 * k + i // 2, 0:P]
                        mm = pe.transpose(bank[:, i * P:(i + 1) * P], src, ident[:])
                    mm.then_inc(t_mm, 1)

            def scores(v, j, unit, ks):
                b, q = j % 2, (j // 2) % 2
                if b == 0 and ks[0] == 0:
                    pe.wait_ge(tp_hi, G * (unit + 1))
                    pe.wait_ge(tp_lo, G * (unit + 1))
                c0 = b * S
                for k in ks:
                    wait(pe, exp_done, 3 * (v - 1) + k + 1)
                    bank = ps_s[:, k, :]
                    if k == 0:
                        w, m = slice(c0, c0 + P), (slice(0, G), slice(c0, c0 + P))
                        masked, heads = bank.rearrange("p (h t) -> p h t", h=G), G
                        out = masked
                    else:
                        w, m = slice(c0 + P, c0 + S), (slice(2 * k - 2, 2 * k), slice(c0, c0 + S))
                        out = bank.rearrange("p (h t) -> p h t", h=2)
                        masked, heads = out[:, :, P:S], 2
                    product3(pe, out, xs[q][0][:, w], xs[q][1][:, w], tp[0][:, m[0], m[1]], tp[1][:, m[0], m[1]],
                             stop=False)
                    pe.matmul(masked, identb[:], mask[:, 0:heads, :], start=False, stop=True,
                              skip_group_check=True).then_inc(s_mm, 1)

            def logits(t, j):
                pe.wait_ge(fx_in, 32 * (t + 1))
                product3(pe, ps_tu[:, 0, :], fx[0][:], fx[1][:], phiT[0][:, j * BK:(j + 1) * BK],
                         phiT[1][:, j * BK:(j + 1) * BK]).then_inc(lg_mm, 1)

            def dispatch(t, j):
                if j == 0:
                    pe.wait_ge(fxn_in, 16 * (t + 1))
                pe.wait_ge(d_norm, 4 * t + j + 1)
                if not live(t + 1, NTT):
                    wait(pe, xt_out, 4 * t + j)
                pe.matmul(ps_tu[:, 1, :], fxn[:], bank_of(disp, t, j), start=True, stop=True).then_inc(xt_mm, 1)

            def output(v, j, unit, part):
                b, q = j % 2, (j // 2) % 2
                if part == 0 and b == 0:
                    pe.wait_ge(v_out, 2 * (unit + 1))
                    wait(pe, o_lo, unit)
                for i in range(G):
                    rows, cols = slice((i % 2) * DH, (i % 2 + 1) * DH), slice(i * DH, (i + 1) * DH)
                    if part == 0:
                        if i % 2 == 0:
                            pe.wait_ge(t_out, 3 * v + i // 2 + 1)
                        mm = pe.matmul(ps_o[rows, 0, b * S:(b + 1) * S], v_sb[q][:, 2 * b, cols],
                                       pT[:, i // 2, (i % 2) * S:(i % 2 + 1) * S],
                                       start=(b == 0 and i < 2), stop=False, skip_group_check=True)
                    else:
                        if i == 0:
                            pe.wait_ge(t_out, 3 * v + 3)
                        mm = pe.matmul(ps_o[rows, 0, b * S + P:(b + 1) * S], v_sb[q][:, 2 * b + 1, cols],
                                       pT[:, 2, i * P:(i + 1) * P], start=False, stop=(i >= G - 2),
                                       skip_group_check=True)
                if part == 1:
                    mm.then_inc(av_mm, 1)

            def make_tp(unit, q, g, jobs=range(G)):
                for i in jobs:
                    if i == 0:
                        pe.wait_ge(a_in, 32 * (g + 1))
                        pe.wait_ge(xs_in[q], 32 * (unit // 2 + 1))
                    ring_free(i, unit)
                    product3(pe, ps_tu[:, i % 2, :], a_w[0][:, i * P:(i + 1) * P], a_w[1][:, i * P:(i + 1) * P],
                             xs[q][0][:], xs[q][1][:]).then_inc(tp_mm, 1)

            def make_v(unit, q, g, b):
                bank = 1 - b
                if b == 0:
                    pe.wait_ge(v_in, 32 * (g + 1))
                    wait(pe, xt_out, state["xt"])
                else:
                    wait(pe, lg_out, state["lg"])
                    wait(pe, wo_out, unit - 1)
                for i in range(2):
                    w = slice((2 * b + i) * P, (2 * b + i + 1) * P)
                    mm = product3(pe, ps_tu[:, bank, i * GV:(i + 1) * GV], xs[q][0][:, w], xs[q][1][:, w],
                                  v_w[0][:], v_w[1][:])
                mm.then_inc(v_mm, 1)

            def times_wo(unit):
                pe.wait_ge(wo_in, 32 * (unit // NPAIR + 1))
                pe.wait_ge(o_hi, unit + 1)
                pe.wait_ge(o_lo, unit + 1)
                wait(pe, lg_out, state["lg"])
                wait(pe, wo_out, unit)
                product3(pe, ps_tu[:, 0, :], wo_w[0][:], wo_w[1][:], o_t[0][:], o_t[1][:]).then_inc(wo_mm, 1)

            state = {}

            def ring_free(i, unit):
                if i == 0:
                    wait(pe, lg_out, state["lg"])
                elif i == 1:
                    wait(pe, xt_out, state["xt"])
                else:
                    pe.wait_ge(tp_hi, G * unit + i - 1)
                    pe.wait_ge(tp_lo, G * unit + i - 1)

            def step(it, j):
                v = 4 * it + j
                unit = 2 * it + j // 2
                for ks in ((0, 1), (2,)):
                    if live(v - 2, NV):
                        transposes(v - 2, j % 2, ks)
                    if live(v, NV):
                        scores(v, j, unit, (0,) if ks[0] == 0 else (1, 2))
                made = unit if not isinstance(unit, int) else min(unit, NU - 1)
                if j % 2 == 0:
                    wait(pe, tp_hi, G * (made + 1))
                    wait(pe, tp_lo, G * (made + 1))
                else:
                    wait(pe, v_out, 2 * (made + 1))
                if live(it, NTT):
                    logits(it, j)
                if live(it - 1, NTT):
                    dispatch(it - 1, j)
                state["lg"] = 4 * it + j + 1 if live(it, NTT) else 4 * NTT
                state["xt"] = 4 * (it - 1) + j + 1 if live(it - 1, NTT) else 0
                for part in range(2):
                    if live(v - 2, NV):
                        output(v - 2, (j + 2) % 4, unit - 1, part)
                    if j % 2 == 1 and live(unit + 1, NU):
                        make_tp(unit + 1, (j // 2 + 1) % 2, (2 * it + j // 2 + 1) // NPAIR, (2 * part, 2 * part + 1))
                    if j % 2 == 0 and part == 0 and live(unit - 2, NU):
                        times_wo(unit - 2)
                    if j % 2 == 0 and live(unit, NU):
                        make_v(unit, (j // 2) % 2, (2 * it + j // 2) // NPAIR, part)

            state["lg"] = state["xt"] = 0
            make_tp(0, 0, 0)
            run(pe, step)

        @block.scalar
        def _(act):
            def transposed_out(v, q):
                if live(v, NV):
                    for k in range(3):
                        act.wait_ge(t_mm, 3 * v + k + 1)
                        wait(act, av_mm, v)
                        nc.scalar.activation(pT[:, k, :], ps_t[:, (q + k) % 2, :], ACT.Copy).then_inc(t_out, 1)

            def softmax_exp(v, j):
                q = j % 2
                wait(act, t_mm, 3 * (v - 1))
                for k in range(3):
                    act.wait_ge(max_done, 3 * v + k + 1)
                    if k == 0:
                        wait(act, inv_done, v - 1)
                    for i in range(G if k == 0 else 2):
                        h = i if k == 0 else 2 * (k - 1) + i
                        c = h if k == 0 else G + h
                        width = P if k == 0 else S
                        dst = e0[q][:, h, :] if k == 0 else e1[q][:, h, :]
                        ins = nc.scalar.activation(dst, ps_s[:, k, i * width:(i + 1) * width], ACT.Exp,
                                                   bias=neg_max[:, q, c:c + 1], accum_out=total[:, q, c:c + 1])
                    ins.then_inc(exp_done, 1)

            def step(it, j):
                v = 4 * it + j
                unit = 2 * it + j // 2
                if j % 2 == 0 and live(unit - 2, NU):
                    act.wait_ge(av_mm, 2 * (unit - 1))
                    wait(act, wo_mm, unit - 2)
                    nc.scalar.activation(o_t[0][:], ps_o[:, 0, :], ACT.Copy).then_inc(o_hi, 1)
                t, jj = step_before(it, j)
                if live(t, NTT):
                    act.wait_ge(d_sub, 4 * t + jj + 1)
                    bank = bank_of(disp, t, jj)
                    nc.scalar.activation(bank, bank, ACT.Exp).then_inc(d_exp, 1)
                transposed_out(v - 2, j % 2)
                if live(v, NV):
                    softmax_exp(v, j)
                if live(it - 1, NTT):
                    act.wait_ge(c_sub, 4 * (it - 1) + j + 1)
                    bank = bank_of(logit, it - 1, j)
                    nc.scalar.activation(bank, bank, ACT.Exp).then_inc(c_exp, 1)
                for part in range(2):
                    two = (2 * part, 2 * part + 1)
                    if j % 2 == 1 and live(unit + 1, NU):
                        take_tp(unit + 1, two)
                    if j % 2 == 0 and live(unit, NU):
                        act.wait_ge(v_mm, 2 * unit + part + 1)
                        wait(act, av_mm, 2 * (unit - 1))
                        nc.scalar.activation(v_sb[(j // 2) % 2][:, two[0]:two[1] + 1, :],
                                             ps_tu[:, 1 - part, :].rearrange("p (t n) -> p t n", t=2),
                                             ACT.Copy).then_inc(v_out, 1)

            def take_tp(unit, jobs=range(G)):
                wait(act, s_mm, 6 * unit)
                for i in jobs:
                    act.wait_ge(tp_mm, G * unit + i + 1)
                    nc.scalar.activation(tp[0][:, i, :], ps_tu[:, i % 2, :], ACT.Copy).then_inc(tp_hi, 1)

            take_tp(0)
            run(act, step)

        @block.vector
        def _(dve):
            def bank_max(v, j):
                q = j % 2
                for k in range(3):
                    dve.wait_ge(s_mm, 3 * v + k + 1)
                    if k == 0:
                        wait(dve, exp_done, 3 * (v - 1))
                    heads = G if k == 0 else 2
                    c = 0 if k == 0 else G + 2 * (k - 1)
                    nc.vector.tensor_reduce(neg_max[:, q, c:c + heads],
                                            ps_s[:, k, :].rearrange("p (h t) -> p h t", h=heads),
                                            AX.X, ALU.max, negate=True).then_inc(max_done, 1)

            def take_tp_lo(unit):
                for i in range(G):
                    dve.wait_ge(tp_hi, G * unit + i + 1)
                    nc.vector.tensor_tensor(tp[1][:, i, :], ps_tu[:, i % 2, :], f32(tp[0][:, i, :]),
                                            ALU.subtract).then_inc(tp_lo, 1)

            def step(it, j):
                v = 4 * it + j
                unit = 2 * it + j // 2
                t = it - 1
                if j % 2 == 0 and live(unit - 2, NU):
                    dve.wait_ge(o_hi, unit - 1)
                    nc.vector.tensor_tensor(o_t[1][:], ps_o[:, 0, :], f32(o_t[0][:]), ALU.subtract).then_inc(o_lo, 1)
                dispatch_sums(*step_before(it, j))
                if live(v, NV):
                    bank_max(v, j)
                if live(it, NTT):
                    take_logits(it, j)
                if live(it - 1, NTT):
                    t = it - 1
                    dve.wait_ge(xt_mm, 4 * t + j + 1)
                    wait(dve, xt_out, 4 * (t - 1) + j + 1)
                    acc = xt_acc[:, j * BK:(j + 1) * BK]
                    nc.vector.tensor_tensor(acc, ps_tu[:, 1, :], acc, ALU.add).then_inc(xt_out, 1)
                if live(it, NTT):
                    bank_maxima(it, j)
                if live(v, NV):
                    dve.wait_ge(exp_done, 3 * v + 3)
                    wait(dve, norm_done, v - 1)
                    nc.vector.reciprocal(inv[:, j % 2, :], total[:, j % 2, :]).then_inc(inv_done, 1)
                if j % 2 == 0 and live(unit - 2, NU):
                    dve.wait_ge(wo_mm, unit - 1)
                    wait(dve, wo_out, unit - 2)
                    o = o_acc[:, bass.ds(((unit - 2) % NPAIR) * PT, PT)]
                    nc.vector.tensor_tensor(o, ps_tu[:, 0, :], o, ALU.add).then_inc(wo_out, 1)
                if j % 2 == 1 and live(unit + 1, NU):
                    take_tp_lo(unit + 1)
                if live(it - 1, NTT):
                    combine_sums(it - 1, j)

            def carry_wait(c, j):
                nc.vector.memset(spare[:, 4 * c + j:4 * c + j + 1], 0.0)

            def take_logits(t, j):
                if isinstance(t, int) and t == 0 and j == 0:
                    dve.wait_ge(bias_in, 16)
                dve.wait_ge(lg_mm, 4 * t + j + 1)
                wait(dve, c_bank, 4 * (t - 2) + j + 1)
                nc.vector.tensor_tensor(bank_of(logit, t, j), ps_tu[:, 0, :], bias[:, j * BK:(j + 1) * BK],
                                        ALU.add).then_inc(lg_out, 1)

            def bank_maxima(t, j):
                n = 4 * t + j
                bank = by_expert(bank_of(logit, t, j))
                dve.wait_ge(lg_out, n + 1)
                wait(dve, d_sub, n - 3)
                wait(dve, m_done, t)
                carry_wait(0, j)
                nc.vector.tensor_reduce(gmax[:, j, :], bank, AX.X, ALU.max).then_inc(g_done, 1)
                nc.vector.tensor_reduce(m_part[:, j, :], bank.rearrange("p e s -> p s e"), AX.X,
                                        ALU.max).then_inc(m_bank, 1)
                if j == 3:
                    dve.wait_ge(m_bank, 4 * (t + 1))
                    carry_wait(1, j)
                    nc.vector.tensor_reduce(m_all[:, bass.ds(t * NP_, NP_)], m_part[:].rearrange("p j s -> p s j"),
                                            AX.X, ALU.max).then_inc(m_done, 1)

            def dispatch_sums(t, j):
                if live(t, NTT):
                    n = 4 * t + j
                    dve.wait_ge(d_exp, n + 1)
                    carry_wait(2, j)
                    nc.vector.tensor_reduce(dsum[:, j, :], by_expert(bank_of(disp, t, j)), AX.X,
                                            ALU.add).then_inc(d_sum, 1)
                    dve.wait_ge(d_sum, n + 1)
                    wait(dve, d_norm, n - 3)
                    nc.vector.reciprocal(dinv[:, j, :], dsum[:, j, :]).then_inc(d_inv, 1)

            def combine_sums(t, j):
                n = 4 * t + j
                dve.wait_ge(c_exp, n + 1)
                wait(dve, c_sum, t)
                carry_wait(3, j)
                nc.vector.tensor_reduce(c_part[:, j, :], by_expert(bank_of(logit, t, j)).rearrange("p e s -> p s e"),
                                        AX.X, ALU.add).then_inc(c_bank, 1)
                if j == 3:
                    dve.wait_ge(c_bank, n + 1)
                    carry_wait(4, j)
                    nc.vector.tensor_reduce(c_all[:, bass.ds(t * NP_, NP_)], c_part[:].rearrange("p j s -> p s j"),
                                            AX.X, ALU.add).then_inc(c_sum, 1)

            take_tp_lo(0)
            run(dve, step)

        @block.gpsimd
        def _(pool):
            def carry_wait(c, j):
                nc.gpsimd.tensor_tensor(pool_spare[:, 4 * c + j:4 * c + j + 1], pool_spare[:, 12:13], pool_spare[:, 13:14], ALU.mult)

            nc.gpsimd.memset(pool_spare[:], 0.0)
            pool.drain()

            def step(it, j):
                v = 4 * it + j
                if live(it - 1, NTT):
                    t = it - 1
                    pool.wait_ge(m_done, t + 1)
                    carry_wait(0, j)
                    bank = by_expert(bank_of(logit, t, j))
                    nc.gpsimd.tensor_tensor(bank, bank, m_all[:, bass.ds(t * NP_, NP_)].unsqueeze(1)
                                            .to_broadcast([P, EB, NP_]), ALU.subtract).then_inc(c_sub, 1)
                t, jj = step_before(it, j)
                if live(t, NTT):
                    pool.wait_ge(d_inv, 4 * t + jj + 1)
                    carry_wait(1, j)
                    bank = by_expert(bank_of(disp, t, jj))
                    nc.gpsimd.tensor_tensor(bank, bank, dinv[:, jj, :].unsqueeze(2).to_broadcast([P, EB, NP_]),
                                            ALU.mult).then_inc(d_norm, 1)
                if live(it, NTT):
                    pool.wait_ge(g_done, 4 * it + j + 1)
                    wait(pool, xt_mm, 4 * (it - 2) + j + 1)
                    carry_wait(2, j)
                    nc.gpsimd.tensor_tensor(by_expert(bank_of(disp, it, j)), by_expert(bank_of(logit, it, j)),
                                            gmax[:, j, :].unsqueeze(2).to_broadcast([P, EB, NP_]),
                                            ALU.subtract).then_inc(d_sub, 1)
                if live(v, NV):
                    q = j % 2
                    pool.wait_ge(inv_done, v + 1)
                    nc.gpsimd.tensor_tensor(e0[q][:], e0[q][:], inv[:, q, 0:G].unsqueeze(2)
                                            .to_broadcast([P, G, P]), ALU.mult)
                    nc.gpsimd.tensor_tensor(e1[q][:], e1[q][:], inv[:, q, G:2 * G].unsqueeze(2)
                                            .to_broadcast([P, G, S]), ALU.mult).then_inc(norm_done, 1)

            run(pool, step)


def experts_phase(nc, env):
    with ExitStack() as ctx:
        def sb(name, shape, dt=F32):
            return ctx.enter_context(nc.sbuf_tensor(name, shape, dt))

        def sem(name):
            return ctx.enter_context(nc.semaphore(name))

        ew = sb("ew", [P, NE, D])
        eb = sb("eb", [P, NST, D])
        xslot = sb("xslot", [P, NST, D])
        xhT = sb("xhT", [P, NS_])
        stats = sb("stats2", [P, NST, 6])
        mv = sb("mv2", [P, NST, 2])
        var, root, quot, rstd = (sb(n, [P, NST]) for n in ("var2", "root2", "quot2", "rstd2"))
        ln_c = sb("ln_c", [P, NTT * NP_])
        lse_parts = sb("lse_parts", [P, NTT, 2, NP_], F32R)
        ps = ctx.enter_context(nc.psum_tensor("ps_e", [P, 8, BK], F32))

        ew_in, eb_in = sem("ew_in"), sem("eb_in")
        clip_done, xs_mm, xs_out, ln2, root_done, xhat, th = (
            sem(n) for n in ("clip_done", "xs_mm", "xs_out", "ln2", "root_done", "xhat", "th"))
        xh_mm, xh_out, y_mm, y_out = (sem(n) for n in ("xh_mm", "xh_out", "y_mm", "y_out"))
        lnc_done, lse_done, lse_split, lt_mm, lt_out = (
            sem(n) for n in ("lnc_done", "lse_done", "lse_split", "lt_mm", "lt_out"))
        ident, xt_acc, m_all, c_all = env["ident"], env["xt_acc"], env["m_all"], env["c_all"]
        y_t, lseT = env["y_t"], env["lseT"]
        NQ = NST // 4
        NL = NTT // 4

        block = ctx.enter_context(nc.Block())

        @block.sync
        def _(sp):
            sp.dma_start(ew[:], env["expert_w"].rearrange("n d h -> d n h")).then_inc(ew_in, 16)
            per_tile = env["expert_b"].rearrange("(t r) h -> r t h", r=4)
            for r in range(4):
                sp.dma_start(eb[NP_ * r:NP_ * (r + 1)], per_tile[r].partition_broadcast(NP_)).then_inc(eb_in, 16)
            sp.wait_ge(ew_in, 16)
            sp.wait_ge(eb_in, 64)

        @block.scalar
        def _(act):
            nc.scalar.activation(ln_c[:], c_all[:], ACT.Ln).then_inc(lnc_done, 1)
            for c in range(NQ):
                act.wait_ge(xs_mm, c + 1)
                nc.scalar.activation(xslot[:, 4 * c:4 * c + 4, :], ps[:, c, :], ACT.Copy).then_inc(xs_out, 1)
            act.wait_ge(ln2, 1)
            nc.scalar.activation(root[:], var[:], ACT.Sqrt).then_inc(root_done, 1)
            for c in range(NL):
                act.wait_ge(lt_mm, c + 1)
                nc.scalar.activation(lseT[:, c * BK:(c + 1) * BK], ps[0:2 * NP_, 4 + c % 4, :],
                                     ACT.Copy).then_inc(lt_out, 1)
            for c in range(NQ):
                act.wait_ge(xhat, c + 1)
                part = xslot[:, 4 * c:4 * c + 4, :]
                nc.scalar.activation(part, part, ACT.Tanh).then_inc(th, 1)
            for c in range(NQ):
                act.wait_ge(xh_mm, c + 1)
                nc.scalar.activation(xhT[:, c * BK:(c + 1) * BK], ps[:, c, :], ACT.Copy).then_inc(xh_out, 1)

        @block.vector
        def _(dve):
            nc.vector.tensor_scalar(xt_acc[:], xt_acc[:], -33000.0, 65000.0, ALU.max, ALU.min).then_inc(clip_done, 1)
            dve.wait_ge(lnc_done, 1)
            nc.vector.tensor_tensor(ln_c[:], ln_c[:], m_all[:], ALU.add).then_inc(lse_done, 1)
            dve.wait_ge(lse_done, 1)
            by_tile = ln_c[:].rearrange("p (t s) -> p t s", s=NP_)
            nc.vector.tensor_copy(lse_parts[:, :, 0, :], by_tile).then_inc(lse_split, 1)
            dve.wait_ge(lse_split, 1)
            nc.vector.tensor_tensor(lse_parts[:, :, 1, :], by_tile, f32(lse_parts[:, :, 0, :]),
                                    ALU.subtract).then_inc(lse_split, 1)
            for t in range(NST):
                if t % 4 == 0:
                    dve.wait_ge(xs_out, t // 4 + 1)
                nc.vector.bn_stats(stats[:, t, :], xslot[:, t, :])
            dve.drain()
            for t in range(NST):
                nc.vector.bn_aggr(mv[:, t, :], stats[:, t, :])
            dve.drain()
            nc.vector.tensor_scalar(var[:], mv[:, :, 1], EPS, None, ALU.add).then_inc(ln2, 1)
            dve.wait_ge(root_done, 1)
            nc.vector.reciprocal(quot[:], root[:]).then_inc(ln2, 1)
            dve.wait_ge(ln2, 2)
            nc.vector.tensor_tensor(quot[:], quot[:], var[:], ALU.mult).then_inc(ln2, 1)
            dve.wait_ge(ln2, 3)
            nc.vector.tensor_tensor(quot[:], quot[:], root[:], ALU.add).then_inc(ln2, 1)
            dve.wait_ge(ln2, 4)
            nc.vector.tensor_scalar(quot[:], quot[:], 0.5, None, ALU.mult).then_inc(ln2, 1)
            dve.wait_ge(ln2, 5)
            nc.vector.reciprocal(rstd[:], quot[:]).then_inc(ln2, 1)
            dve.wait_ge(ln2, 6)
            for t in range(NST):
                ins = nc.vector.tensor_scalar(xslot[:, t, :], xslot[:, t, :], mv[:, t, 0:1], rstd[:, t:t + 1],
                                              ALU.subtract, ALU.mult)
                if t % 4 == 3:
                    ins.then_inc(xhat, 1)
            dve.wait_ge(eb_in, 64)
            for c in range(NQ):
                dve.wait_ge(y_mm, c + 1)
                part = slice(4 * c, 4 * c + 4)
                nc.vector.tensor_tensor(eb[:, part, :], ps[:, 4 + c, :].rearrange("p (t h) -> p t h", t=4),
                                        eb[:, part, :], ALU.add).then_inc(y_out, 1)
                dve.wait_ge(y_out, 3 * c + 1)
                nc.vector.tensor_copy(y_t[0][:, part, :], eb[:, part, :]).then_inc(y_out, 1)
                dve.wait_ge(y_out, 3 * c + 2)
                nc.vector.tensor_tensor(y_t[1][:, part, :], eb[:, part, :], f32(y_t[0][:, part, :]),
                                        ALU.subtract).then_inc(y_out, 1)

        @block.tensor
        def _(pe):
            pe.wait_ge(clip_done, 1)
            for t in range(NST):
                mm = pe.transpose(ps[:, t // 4, (t % 4) * P:(t % 4 + 1) * P], xt_acc[:, t * P:(t + 1) * P], ident[:])
                if t % 4 == 3:
                    mm.then_inc(xs_mm, 1)
            pe.wait_ge(lse_split, 2)
            for t in range(NTT):
                if t % 4 == 0 and t >= 16:
                    pe.wait_ge(lt_out, t // 4 - 3)
                mm = pe.transpose(ps[0:2 * NP_, 4 + (t // 4) % 4, (t % 4) * P:(t % 4 + 1) * P],
                                  f32(lse_parts[:, t, :, :].rearrange("p a b -> p (a b)")), ident[:])
                if t % 4 == 3:
                    mm.then_inc(lt_mm, 1)
            for t in range(NST):
                if t % 4 == 0:
                    pe.wait_ge(th, t // 4 + 1)
                mm = pe.transpose(ps[:, t // 4, (t % 4) * P:(t % 4 + 1) * P], xslot[:, t, :], ident[:])
                if t % 4 == 3:
                    mm.then_inc(xh_mm, 1)
            pe.wait_ge(ew_in, 16)
            pe.wait_ge(lt_out, NL)
            for t in range(NST):
                if t % 4 == 0:
                    pe.wait_ge(xh_out, t // 4 + 1)
                for r in range(4):
                    mm = pe.matmul(ps[NP_ * r:NP_ * (r + 1), 4 + t // 4, (t % 4) * P:(t % 4 + 1) * P],
                                   xhT[:, t * P + NP_ * r:t * P + NP_ * (r + 1)], ew[:, 4 * t + r, :],
                                   start=True, stop=True, skip_group_check=True)
                if t % 4 == 3:
                    mm.then_inc(y_mm, 1)


def combine_phase(nc, env):
    with ExitStack() as ctx:
        def sb(name, shape, dt=F32):
            return ctx.enter_context(nc.sbuf_tensor(name, shape, dt))

        def psum(name, banks):
            return ctx.enter_context(nc.psum_tensor(name, [P, banks, BK], F32))

        def sem(name):
            return ctx.enter_context(nc.semaphore(name))

        R = 4
        LAG = 2
        cT = sb("cT", [P, R, BK])
        c_hi, c_lo = (sb(n, [P, R, BK], F32R) for n in ("c_hi", "c_lo"))
        fin = sb("fin", [P, PT])
        xres = sb("xres", [P, 2, 4, D])
        res = sb("res", [P, 2, 4, D])
        ps_l, ps_y, ps_f = psum("ps_l", R), psum("ps_y", 2), psum("ps_f", 1)
        lt_mm, c_exp, c_low, y_mm, fin_done, f_mm, res_done = (
            sem(n) for n in ("lt2_mm", "c2_exp", "c2_low", "y2_mm", "fin_done", "f_mm", "res_done"))
        x_in = [sem("x_in0"), sem("x_in1")]
        stored = [sem("stored0"), sem("stored1")]
        ident, xT, phiT, nsel, lseT = env["ident"], env["xT"], env["phiT"], env["nsel"], env["lseT"]
        y_t, phibT, o_acc = env["y_t"], env["phibT"], env["o_acc"]
        x_pair = env["x"].rearrange("(n t p) d -> n p t d", p=P, t=4)
        out_pair = env["out"].rearrange("(n t p) d -> n p t d", p=P, t=4)

        block = ctx.enter_context(nc.Block())

        @block.sync
        def _(sp):
            for p in range(NPAIR):
                wait(sp, res_done, p - 1)
                sp.dma_start(xres[:, p % 2], x_pair[p]).then_inc(x_in[p % 2], 16)

        @block.gpsimd
        def _(pool):
            for p in range(NPAIR):
                pool.wait_ge(res_done, p + 1)
                pool.dma_start(out_pair[p], res[:, p % 2]).then_inc(stored[p % 2], 16)
            for q in range(2):
                pool.wait_ge(stored[q], 16 * NPAIR // 2)

        @block.tensor
        def _(pe):
            def untranspose(p):
                pe.wait_ge(fin_done, p + 1)
                wait(pe, res_done, p)
                for i in range(4):
                    mm = pe.transpose(ps_f[:, 0, i * P:(i + 1) * P], fin[:, i * P:(i + 1) * P], ident[:])
                mm.then_inc(f_mm, 1)

            def logits_t(p, st):
                n = NST * p + st
                w, tok = slice(st * P, (st + 1) * P), bass.ds(p * PT, PT)
                wait(pe, c_exp, n - R + 1)
                product3(pe, ps_l[:, st % R, :], phiT[0][:, w], phiT[1][:, w], xT[0][:, tok], xT[1][:, tok],
                         stop=False)
                pe.matmul(ps_l[:, st % R, :], nsel[:], lseT[:, tok], start=False, stop=True,
                          skip_group_check=True).then_inc(lt_mm, 1)

            def mix(p, q, st):
                pe.wait_ge(c_low, NST * p + st + 1)
                if st == 0:
                    wait(pe, fin_done, p - 1)
                product3(pe, ps_y[:, q, :], y_t[0][:, st, :], y_t[1][:, st, :], c_hi[:, st % R, :],
                         c_lo[:, st % R, :], start=(st == 0), stop=(st == NST - 1)).then_inc(y_mm, 1)

            def pair(p, q):
                for st in range(NST):
                    logits_t(p, st)
                    if st >= LAG:
                        mix(p, q, st - LAG)
                    elif live(p - 1, NPAIR):
                        mix(p - 1, 1 - q, NST + st - LAG)
                    if st == 6 and live(p - 1, NPAIR):
                        untranspose(p - 1)

            pair(0, 0)
            pair(1, 1)
            with pe.Fori(1, NPAIR // 2) as pp:
                for q in range(2):
                    pair(2 * pp + q, q)
            for st in range(NST - LAG, NST):
                mix(NPAIR - 1, 1, st)
            untranspose(NPAIR - 1)

        @block.scalar
        def _(act):
            def pair(p):
                for st in range(NST):
                    act.wait_ge(lt_mm, NST * p + st + 1)
                    wait(act, y_mm, NST * p + st - R + 1)
                    nc.scalar.activation(c_hi[:, st % R, :], ps_l[:, st % R, :], ACT.Exp, bias=phibT[:, st:st + 1])
                    nc.scalar.activation(cT[:, st % R, :], ps_l[:, st % R, :], ACT.Exp,
                                         bias=phibT[:, st:st + 1]).then_inc(c_exp, 1)

            pair(0)
            with act.Fori(1, NPAIR) as p:
                pair(p)

        @block.vector
        def _(dve):
            def add_x(p):
                dve.wait_ge(f_mm, p + 1)
                dve.wait_ge(x_in[p % 2], 16 * (p // 2 + 1))
                wait(dve, stored[p % 2], 16 * (p // 2))
                nc.vector.tensor_tensor(res[:, p % 2], ps_f[:, 0, :].rearrange("p (t d) -> p t d", t=4),
                                        xres[:, p % 2], ALU.add).then_inc(res_done, 1)

            def low_parts(p, tiles):
                for st in tiles:
                    dve.wait_ge(c_exp, NST * p + st + 1)
                    wait(dve, y_mm, NST * p + st - R + 1)
                    nc.vector.tensor_tensor(c_lo[:, st % R, :], cT[:, st % R, :], f32(c_hi[:, st % R, :]),
                                            ALU.subtract).then_inc(c_low, 1)

            def finish(p):
                dve.wait_ge(y_mm, NST * (p + 1))
                wait(dve, f_mm, p)
                nc.vector.tensor_tensor(fin[:], ps_y[:, p % 2, :], o_acc[:, p * PT:(p + 1) * PT],
                                        ALU.add).then_inc(fin_done, 1)

            EARLY = 3
            for p in range(NPAIR + 1):
                if p < NPAIR:
                    low_parts(p, range(EARLY))
                if p > 0:
                    finish(p - 1)
                if p < NPAIR:
                    low_parts(p, range(EARLY, 8))
                if p > 0:
                    add_x(p - 1)
                if p < NPAIR:
                    low_parts(p, range(8, NST))


def build(nc, x, wq, wk, wv, wo, lq1, lk1, lq2, lk2, phi_w, phi_b, expert_w, expert_b, out):
    with ExitStack() as ctx:
        def sb(name, shape, dt=F32):
            return ctx.enter_context(nc.sbuf_tensor(name, shape, dt))

        env = dict(x=x.rearrange("b s d -> (b s) d"), wq=wq, wk=wk, wv=wv, wo=wo, lq1=lq1, lk1=lk1, lq2=lq2, lk2=lk2,
                   phi_w=phi_w, phi_b=phi_b, expert_w=expert_w, expert_b=expert_b,
                   out=out.rearrange("b s d -> (b s) d"))
        env["a_dram"] = nc.dram_tensor("a_scratch", [NG, 2, P, G * P], F32, kind="Internal").ap()
        env["v_dram"] = nc.dram_tensor("v_scratch", [NG, 2, P, GV], F32, kind="Internal").ap()
        env["wo_dram"] = nc.dram_tensor("wo_scratch", [NG, 2, P, D], F32, kind="Internal").ap()
        env["xn_dram"] = nc.dram_tensor("xn_scratch", [NTT, P, D], F32, kind="Internal").ap()
        env["ident"] = sb("ident", [P, P])
        env["identb"] = sb("identb", [P, P], BF16)
        env["mask"] = sb("mask", [P, G, P], BF16)
        env["xT"] = [sb(f"xT{h}", [P, NT], F32R) for h in range(2)]
        env["phiT"] = [sb(f"phiT{h}", [P, NS_], F32R) for h in range(2)]
        env["phibT"] = sb("phibT", [P, NST])
        env["nsel_f"] = sb("nsel_f", [2 * NP_, P])
        env["nsel"] = sb("nsel", [2 * NP_, P], F32R)
        env["o_acc"] = sb("o_acc", [P, NT])
        env["xt_acc"] = sb("xt_acc", [P, NS_])
        env["m_all"] = sb("m_all", [P, NTT * NP_])
        env["c_all"] = sb("c_all", [P, NTT * NP_])
        setup_phase(nc, env)
        main_phase(nc, env)
        env["y_t"] = [sb(f"y_t{h}", [P, NST, D], F32R) for h in range(2)]
        env["lseT"] = sb("lseT", [2 * NP_, NT], F32R)
        experts_phase(nc, env)
        combine_phase(nc, env)


_INS = ["L0_attn_x", "L0_attn_Wq", "L0_attn_Wk", "L0_attn_Wv", "L0_attn_Wo", "L0_attn_lq1", "L0_attn_lk1",
        "L0_attn_lq2", "L0_attn_lk2", "L0_ffn_phi_w", "L0_ffn_phi_b", "L0_ffn_expert_w", "L0_ffn_expert_b"]


def kernel(**inputs):
    import concourse.bacc as bacc
    from concourse.bass_utils import run_bass_kernel_spmd as run

    nc = bacc.Bacc("TRN2", target_bir_lowering=False, num_devices=1)
    arrays, args = {}, []
    for name in _INS:
        a = np.ascontiguousarray(inputs[name])
        arrays[f"in_{name}"] = a
        args.append(nc.dram_tensor(f"in_{name}", a.shape, mybir.dt.from_np(a.dtype), kind="ExternalInput").ap())
    out = nc.dram_tensor("out_dram", (NB, S, D), F32, kind="ExternalOutput").ap()
    build(nc, *args, out)
    r = run(nc, [arrays], core_ids=[0])
    return r.results[0]["out_dram"]
```

```python
from contextlib import ExitStack

import numpy as np

import concourse.bass as bass
from concourse import mybir
from concourse.alu_op_type import AluOpType as ALU

F32 = mybir.dt.float32
F32R = mybir.dt.float32r
BF16 = mybir.dt.bfloat16
ACT = mybir.ActivationFunctionType
AX = mybir.AxisListType

P = 128
NB, S, D = 16, 256, 128
NT = NB * S
NTT = NT // P
DH = 64
NH = 16
NHH = 2 * NH
G = 4
NG = NHH // G
GV = G * DH
NPAIR = NB // 2
PT = 2 * S
NU = NG * NPAIR
NV = 2 * NU
NE, NP_, NS_ = 64, 32, 2048
NST = NS_ // P
BK = 512
EB = BK // NP_
LAMBDA_INIT = 0.8
OUT_SCALE = 1.0 - LAMBDA_INIT
SCORE_SCALE = DH ** -0.5
EPS = 1e-5
MASKED = -1e30
ITER = NTT


def wait(eng, sem, value):
    if isinstance(value, int) and value <= 0:
        return
    eng.wait_ge(sem, value)


def head_half(g, i):
    return NH * (i // 2) + 4 * (g // 2) + 2 * (i % 2) + g % 2


def live(i, n):
    return not isinstance(i, int) or 0 <= i < n


def f32(ap):
    return ap.bitcast(F32)


def product3(pe, out, w_hi, w_lo, m_hi, m_lo, start=True, stop=True):
    pe.matmul(out, w_hi, m_hi, start=start, stop=False, skip_group_check=True)
    pe.matmul(out, w_hi, m_lo, start=False, stop=False, skip_group_check=True)
    return pe.matmul(out, w_lo, m_hi, start=False, stop=stop, skip_group_check=True)


def setup_phase(nc, env):
    NBANK = 6
    with ExitStack() as ctx:
        def sb(name, shape, dt=F32):
            return ctx.enter_context(nc.sbuf_tensor(name, shape, dt))

        def sem(name):
            return ctx.enter_context(nc.semaphore(name))

        wq, wk, wv = (sb(n, [P, NHH * DH]) for n in ("wq", "wk", "wv"))
        wo = sb("wo", [P, NG, D])
        v_parts = [sb(f"v_part{h}", [P, NG * GV], F32R) for h in range(2)]
        wo_parts = [sb(f"wo_part{h}", [P, NG, D], F32R) for h in range(2)]
        phi_w = sb("phi_w", [P, NST, D])
        wT = {n: sb(n + "T", [P, NHH * DH]) for n in ("wq", "wk")}
        stage = sb("stage", [P, 4, 2, BK], F32R)
        lqk = sb("lqk", [P, 4, DH])
        lprod = sb("lprod", [P, 2, DH])
        ldot = sb("ldot", [P, 2])
        lexp = sb("lexp", [P, 2])
        lam = sb("lam", [P, 1])
        neg_lam = sb("neg_lam", [P, 1])
        stats = sb("stats", [P, NTT, 6])
        mv = sb("mv", [P, NTT, 2])
        var = sb("var", [P, NTT])
        root = sb("root", [P, NTT])
        rstd = sb("rstd", [P, NTT])
        quot = sb("quot", [P, NTT])
        shift = sb("shift", [P, NTT])
        phib_rows = sb("phib_rows", [NST, P])
        ps = ctx.enter_context(nc.psum_tensor("ps_setup", [P, NBANK, BK], F32))
        ps_b = ctx.enter_context(nc.psum_tensor("ps_phib", [P, BK], F32))

        loaded = {n: sem("loaded_" + n) for n in ("x", "phi", "wq", "wk", "wv", "wo", "l", "phib")}
        s_const = sem("s_const")
        job_done = sem("job_done")
        hi_out = sem("hi_out")
        lo_out = sem("lo_out")
        ln_step = sem("ln_step")
        var_root = sem("var_root")
        xn_ready = sem("xn_ready")
        lam_step = sem("lam_step")
        lam_exp = sem("lam_exp")
        w_hi, w_lo = sem("w_hi"), sem("w_lo")
        a_stored = [sem(f"a_stored{i}") for i in range(4)]
        w_stored = sem("w_stored")
        phib_done = sem("phib_done")
        phib_out = sem("phib_out")

        ident, identb, mask = env["ident"], env["identb"], env["mask"]
        xT, phiT = env["xT"], env["phiT"]
        a_dram, v_dram, wo_dram, x_sb = env["a_dram"], env["v_dram"], env["wo_dram"], env["xn"]

        jobs = [("wq", i) for i in range(4)] + [("wk", i) for i in range(4)] + [("A", i) for i in range(NG)]
        jobs += [("phi", i) for i in range(4)] + [("x", i) for i in range(8)]
        AHEAD = 8
        SPLIT = ("phi", "x", "A")
        lo_count = [sum(k in SPLIT for k, _ in jobs[:n + 1]) for n in range(len(jobs))]
        at = {job: n for n, job in enumerate(jobs)}

        def parts(kind, i):
            if kind == "phi":
                return [t[:, i * BK:(i + 1) * BK] for t in phiT]
            if kind == "x":
                return [t[:, i * BK:(i + 1) * BK] for t in xT]
            return [stage[:, i % 4, h, :] for h in range(2)]

        def wv_quarters():
            for half in range(2):
                for r in range(2):
                    src = wv[:].rearrange("p (s k h r d) -> p s r k h d", s=2, h=2, r=2, d=DH)[:, half, r]
                    dst = [v[:].rearrange("p (k r s h d) -> p s r k h d", r=2, s=2, h=2, d=DH)[:, half, r]
                           for v in v_parts]
                    yield (OUT_SCALE if half == 0 else neg_lam[:]), src, dst

        block = ctx.enter_context(nc.Block())

        @block.sync
        def _(sp):
            sp.dma_start(x_sb[:], env["x"].rearrange("(t p) d -> p t d", p=P)).then_inc(loaded["x"], 16)
            for i, v in enumerate(("lq1", "lk1", "lq2", "lk2")):
                sp.dma_start(lqk[:, i, :], env[v].partition_broadcast(P)).then_inc(loaded["l"], 16)
            sp.dma_start(phi_w[:], env["phi_w"].rearrange("(t p) d -> p t d", p=P)).then_inc(loaded["phi"], 16)
            sp.dma_start(wv[:], env["wv"]).then_inc(loaded["wv"], 16)
            for h in range(2):
                for r in range(2):
                    sp.dma_start(wo[h * DH:(h + 1) * DH, r::2, :],
                                 env["wo"].rearrange("(k h r d) m -> h r d k m", h=2, r=2, d=DH)[h, r]
                                 ).then_inc(loaded["wo"], 16)
            for i in range(NG):
                sp.wait_ge(hi_out, at[("A", i)] + 1)
                sp.wait_ge(lo_out, lo_count[at[("A", i)]])
                sp.dma_start(a_dram[i].rearrange("h p n -> p h n"), f32(stage[:, i % 4])).then_inc(a_stored[i % 4], 16)
                if i == 3:
                    sp.wait_ge(w_hi, 5)
                    sp.wait_ge(w_lo, 5)
                    for h in range(2):
                        sp.dma_start(v_dram[:, h].rearrange("g p n -> p g n"),
                                     f32(v_parts[h][:]).rearrange("p (g n) -> p g n", g=NG)).then_inc(w_stored, 16)
                        sp.dma_start(wo_dram[:, h].rearrange("g p n -> p g n"), f32(wo_parts[h][:])).then_inc(w_stored, 16)
            for q in range(4):
                sp.wait_ge(a_stored[q], 16 * NG // 4)
            sp.wait_ge(w_stored, 64)

        @block.gpsimd
        def _(pool):
            for t in (ident, identb):
                nc.gpsimd.memset(t[:], 0.0).then_inc(s_const, 1)
            nc.gpsimd.memset(mask[:], 0.0).then_inc(s_const, 1)
            pool.wait_ge(s_const, 3)
            for t in (ident, identb):
                nc.gpsimd.affine_select(out=t[:], in_=t[:], compare_op=ALU.not_equal, fill=1.0, base=0,
                                        pattern=[[-1, P]], channel_multiplier=1).then_inc(s_const, 1)
            nc.gpsimd.affine_select(out=mask[:], in_=mask[:], compare_op=ALU.is_ge, fill=MASKED, base=0,
                                    pattern=[[0, G], [-1, P]], channel_multiplier=1).then_inc(s_const, 1)
            nc.gpsimd.memset(env["o_acc"][:], 0.0)
            nc.gpsimd.memset(env["xt_acc"][:], 0.0)
            nsel = env["nsel_f"]
            nc.gpsimd.memset(nsel[:], 0.0).then_inc(s_const, 1)
            pool.wait_ge(s_const, 7)
            for n, base in enumerate((0, -NP_)):
                nc.gpsimd.affine_select(out=nsel[:], in_=nsel[:], compare_op=ALU.not_equal, fill=-1.0, base=base,
                                        pattern=[[0, P // NP_], [-1, NP_]], channel_multiplier=1).then_inc(s_const, 1)
                pool.wait_ge(s_const, 8 + n)

        @block.scalar
        def _(act):
            act.dma_start(wq[:], env["wq"]).then_inc(loaded["wq"], 16)
            act.dma_start(wk[:], env["wk"]).then_inc(loaded["wk"], 16)
            act.dma_start(phib_rows[:], env["phi_b"].rearrange("(t p) -> t p", p=P)).then_inc(loaded["phib"], 16)

            def take_hi(n):
                kind, i = jobs[n]
                bank = ps[:, n % NBANK, :]
                act.wait_ge(job_done, n + 1)
                if kind in SPLIT:
                    if kind == "A" and i >= 4:
                        act.wait_ge(a_stored[i % 4], 16 * (i // 4))
                    hi = parts(kind, i)[0]
                    if kind == "A":
                        nc.scalar.activation(hi, bank, ACT.Copy, scale=SCORE_SCALE).then_inc(hi_out, 1)
                    else:
                        nc.scalar.activation(hi, bank, ACT.Copy).then_inc(hi_out, 1)
                else:
                    nc.scalar.activation(wT[kind][:, i * BK:(i + 1) * BK], bank, ACT.Copy).then_inc(hi_out, 1)

            for n in range(AHEAD):
                take_hi(n)
            act.wait_ge(ln_step, 1)
            nc.scalar.activation(root[:], var[:], ACT.Sqrt).then_inc(var_root, 1)
            act.wait_ge(lam_step, 2)
            nc.scalar.activation(lexp[:], ldot[:], ACT.Exp).then_inc(lam_exp, 1)
            act.wait_ge(ln_step, 7)
            for t in range(NTT // 2, NTT):
                last = nc.scalar.activation(x_sb[:, t, :], x_sb[:, t, :], ACT.Identity, bias=shift[:, t:t + 1],
                                            scale=rstd[:, t:t + 1])
            last.then_inc(xn_ready, 1)
            for n in range(AHEAD, len(jobs)):
                take_hi(n)
                if jobs[n] == ("A", 3):
                    act.wait_ge(loaded["wo"], 64)
                    nc.scalar.activation(wo_parts[0][:], wo[:], ACT.Copy).then_inc(w_hi, 1)
                    act.wait_ge(loaded["wv"], 16)
                    act.wait_ge(lam_step, 4)
                    for scale, src, dst in wv_quarters():
                        nc.scalar.activation(dst[0], src, ACT.Identity, scale=scale).then_inc(w_hi, 1)
            act.wait_ge(phib_done, 1)
            nc.scalar.activation(env["phibT"][:], ps_b[:, 0:NST], ACT.Copy).then_inc(phib_out, 1)

        @block.vector
        def _(dve):
            dve.wait_ge(loaded["x"], 16)
            for t in range(NTT):
                nc.vector.bn_stats(stats[:, t, :], x_sb[:, t, :])
            dve.drain()
            for t in range(NTT):
                nc.vector.bn_aggr(mv[:, t, :], stats[:, t, :])
            dve.drain()
            nc.vector.tensor_scalar(var[:], mv[:, :, 1], EPS, None, ALU.add).then_inc(ln_step, 1)
            dve.wait_ge(loaded["l"], 64)
            nc.vector.tensor_tensor(lprod[:], lqk[:, 0:4:2, :], lqk[:, 1:4:2, :], ALU.mult).then_inc(lam_step, 1)
            dve.wait_ge(lam_step, 1)
            nc.vector.tensor_reduce(ldot[:], lprod[:], AX.X, ALU.add).then_inc(lam_step, 1)
            dve.wait_ge(var_root, 1)
            nc.vector.reciprocal(quot[:], root[:]).then_inc(ln_step, 1)
            dve.wait_ge(ln_step, 2)
            nc.vector.tensor_tensor(quot[:], quot[:], var[:], ALU.mult).then_inc(ln_step, 1)
            dve.wait_ge(ln_step, 3)
            nc.vector.tensor_tensor(quot[:], quot[:], root[:], ALU.add).then_inc(ln_step, 1)
            dve.wait_ge(ln_step, 4)
            nc.vector.tensor_scalar(quot[:], quot[:], 0.5, None, ALU.mult).then_inc(ln_step, 1)
            dve.wait_ge(ln_step, 5)
            nc.vector.reciprocal(rstd[:], quot[:]).then_inc(ln_step, 1)
            dve.wait_ge(ln_step, 6)
            nc.vector.scalar_tensor_tensor(out=shift[:], in0=mv[:, :, 0], scalar=-1.0, in1=rstd[:], op0=ALU.mult,
                                           op1=ALU.mult).then_inc(ln_step, 1)
            for t in range(NTT // 2):
                last = nc.vector.tensor_scalar(x_sb[:, t, :], x_sb[:, t, :], mv[:, t, 0:1], rstd[:, t:t + 1],
                                               ALU.subtract, ALU.mult)
            last.then_inc(xn_ready, 1)
            dve.wait_ge(lam_exp, 1)
            nc.vector.tensor_tensor(lam[:], lexp[:, 0:1], lexp[:, 1:2], ALU.subtract).then_inc(lam_step, 1)
            dve.wait_ge(lam_step, 3)
            nc.vector.tensor_scalar(neg_lam[:], lam[:], LAMBDA_INIT, -OUT_SCALE, ALU.add, ALU.mult).then_inc(lam_step, 1)
            dve.wait_ge(lam_step, 4)
            dve.wait_ge(s_const, 9)
            nc.vector.tensor_copy(env["nsel"][:], env["nsel_f"][:])
            for n, (kind, i) in enumerate(jobs):
                if kind not in SPLIT:
                    continue
                hi, lo = parts(kind, i)
                scale = SCORE_SCALE if kind == "A" else 1.0
                dve.wait_ge(hi_out, n + 1)
                nc.vector.scalar_tensor_tensor(out=lo, in0=ps[:, n % NBANK, :], scalar=scale, in1=f32(hi),
                                               op0=ALU.mult, op1=ALU.subtract).then_inc(lo_out, 1)
                if (kind, i) == ("A", 3):
                    dve.wait_ge(w_hi, 1)
                    nc.vector.tensor_tensor(wo_parts[1][:], wo[:], f32(wo_parts[0][:]), ALU.subtract).then_inc(w_lo, 1)
                    for n_hi, (scale, src, dst) in enumerate(wv_quarters()):
                        dve.wait_ge(w_hi, n_hi + 2)
                        nc.vector.scalar_tensor_tensor(out=dst[1], in0=src, scalar=scale, in1=f32(dst[0]),
                                                       op0=ALU.mult, op1=ALU.subtract).then_inc(w_lo, 1)

        @block.tensor
        def _(pe):
            pe.wait_ge(s_const, 6)
            need = {"phi": "phi", "wq": "wq", "wk": "wk"}
            for n, (kind, i) in enumerate(jobs):
                if n >= NBANK:
                    pe.wait_ge(hi_out, n - NBANK + 1)
                    wait(pe, lo_out, lo_count[n - NBANK])
                if kind in need and i == 0:
                    pe.wait_ge(loaded[need[kind]], 16)
                if kind == "x" and i == 0:
                    pe.wait_ge(xn_ready, 2)
                if kind == "A" and i == 0:
                    pe.wait_ge(hi_out, at[("wk", 3)] + 1)
                for j in range(4):
                    out = ps[:, n % NBANK, j * P:(j + 1) * P]
                    c = 4 * i + j
                    if kind == "phi":
                        mm = pe.transpose(out, phi_w[:, c, :], ident[:])
                    elif kind == "x":
                        mm = pe.transpose(out, x_sb[:, c, :], ident[:])
                    elif kind in wT:
                        src = {"wq": wq, "wk": wk}[kind]
                        mm = pe.transpose(out, src[:, c * P:(c + 1) * P], ident[:])
                    else:
                        c = head_half(i, j)
                        r0, t0 = (c % 2) * DH, (c // 2) * P
                        rows = slice(r0, r0 + DH)
                        mm = pe.matmul(out, wT["wk"][rows, t0:t0 + P], wT["wq"][rows, t0:t0 + P],
                                       start=True, stop=True, skip_group_check=True)
                mm.then_inc(job_done, 1)
            pe.wait_ge(loaded["phib"], 16)
            pe.transpose(ps_b[:, 0:NST], phib_rows[:], ident[0:NST, 0:NST]).then_inc(phib_done, 1)


def main_phase(nc, env):
    with ExitStack() as ctx:
        def sb(name, shape, dt=F32):
            return ctx.enter_context(nc.sbuf_tensor(name, shape, dt))

        def psum(name, banks):
            return ctx.enter_context(nc.psum_tensor(name, [P, banks, BK], F32))

        def sem(name):
            return ctx.enter_context(nc.semaphore(name))

        xs = [[sb(f"xs{q}{h}", [P, PT], F32R) for h in range(2)] for q in range(2)]
        a_w = [sb(f"a_w{h}", [P, G * P], F32R) for h in range(2)]
        v_w = [sb(f"v_w{h}", [P, GV], F32R) for h in range(2)]
        wo_w = [sb(f"wo_w{h}", [P, D], F32R) for h in range(2)]
        o_t = [sb(f"o_t{h}", [P, PT], F32R) for h in range(2)]
        tp = [sb(f"tp{h}", [P, G, PT], F32R) for h in range(2)]
        v_sb = [sb(f"v_sb{q}", [P, 4, GV]) for q in range(2)]
        e0 = [sb(f"e0{q}", [P, G, P]) for q in range(2)]
        e1 = [sb(f"e1{q}", [P, G, S]) for q in range(2)]
        pT = sb("pT", [P, 3, BK])
        neg_max = sb("neg_max", [P, 2, 2 * G])
        total = sb("total", [P, 2, 2 * G])
        inv = sb("inv", [P, 2, 2 * G])
        fx = [sb(f"fx{h}", [P, P], F32R) for h in range(2)]
        fxn = sb("fxn", [P, D])
        bias = sb("bias", [P, NS_])
        logit = sb("logit", [P, 2 * NS_])
        disp = sb("disp", [P, 2 * NS_])
        gmax = sb("gmax", [P, 4, EB])
        dsum = sb("dsum", [P, 4, EB])
        dinv = sb("dinv", [P, 4, EB])
        m_part = sb("m_part", [P, 4, NP_])
        c_part = sb("c_part", [P, 4, NP_])
        spare = sb("spare", [P, 20])
        pool_spare = sb("pool_spare", [P, 6])
        ps_tu, ps_s, ps_t, ps_o = psum("ps_tu", 2), psum("ps_s", 3), psum("ps_t", 2), psum("ps_o", 1)

        xs_in = [sem("xs_in0"), sem("xs_in1")]
        a_in, v_in, wo_in, fx_in, fxn_in, bias_in = (
            sem(n) for n in ("a_in", "v_in", "wo_in", "fx_in", "fxn_in", "bias_in"))
        tp_mm, v_mm, lg_mm, xt_mm, s_mm, t_mm, av_mm, wo_mm = (
            sem(n) for n in ("tp_mm", "v_mm", "lg_mm", "xt_mm", "s_mm", "t_mm", "av_mm", "wo_mm"))
        tp_hi, tp_lo, v_out, lg_out, xt_out, t_out, o_hi, o_lo, wo_out = (
            sem(n) for n in ("tp_hi", "tp_lo", "v_out", "lg_out", "xt_out", "t_out", "o_hi", "o_lo", "wo_out"))
        max_done, exp_done, inv_done, norm_done = (sem(n) for n in ("max_done", "exp_done", "inv_done", "norm_done"))
        g_done, d_sub, d_exp, d_sum, d_inv, d_norm = (
            sem(n) for n in ("g_done", "d_sub", "d_exp", "d_sum", "d_inv", "d_norm"))
        m_bank, m_done, c_sub, c_exp, c_bank, c_sum = (
            sem(n) for n in ("m_bank", "m_done", "c_sub", "c_exp", "c_bank", "c_sum"))

        def bank_of(buf, t, j):
            return buf[:, bass.ds((t % 2) * NS_ + j * BK, BK)]

        def by_expert(ap):
            return ap.rearrange("p (e s) -> p e s", s=NP_)

        def step_before(it, j):
            return (it, j - 1) if j > 0 else (it - 1, 3)

        ident, identb, mask = env["ident"], env["identb"], env["mask"]
        xT, phiT, o_acc, xt_acc = env["xT"], env["phiT"], env["o_acc"], env["xt_acc"]
        m_all, c_all = env["m_all"], env["c_all"]
        a_dram, v_dram, wo_dram, x_sb = env["a_dram"], env["v_dram"], env["wo_dram"], env["xn"]

        block = ctx.enter_context(nc.Block())

        def run(eng, step):
            for it in range(3):
                for j in range(4):
                    step(it, j)
            with eng.Fori(3, ITER - 1) as it:
                for j in range(4):
                    step(it, j)
            for it in range(ITER - 1, ITER + 1):
                for j in range(4):
                    step(it, j)

        @block.sync
        def _(sp):
            def load_xs(unit, q, pair):
                if not live(unit, NU):
                    return
                wait(sp, s_mm, 3 * (2 * (unit - 2) + 2))
                wait(sp, v_mm, 2 * (unit - 1))
                for h in range(2):
                    sp.dma_start(f32(xs[q][h][:]), f32(xT[h][:, bass.ds(pair * PT, PT)])).then_inc(xs_in[q], 16)

            def load_group(g, w, dram, count, per_unit, s_in):
                wait(sp, count, per_unit * NPAIR * g)
                for h in range(2):
                    sp.dma_start(f32(w[h][:]), dram[g, h]).then_inc(s_in, 16)

            def load_tile(it):
                if live(it, NTT):
                    wait(sp, xt_mm, 4 * it)
                    wait(sp, lg_mm, 4 * (it + 1))
                if live(it + 1, NTT):
                    for h in range(2):
                        sp.dma_start(f32(fx[h][:]), f32(xT[h][:, bass.ds((it + 1) * P, P)])).then_inc(fx_in, 16)
                if live(it, NTT):
                    sp.dma_start(fxn[:], x_sb[:].rearrange("p t d -> p (t d)")[:, bass.ds(it * D, D)]
                                 ).then_inc(fxn_in, 16)

            def iteration(it, kk, g, last=False):
                load_xs(2 * it + 2, 0, (2 * kk + 2) % NPAIR)
                if kk == 0 and not (isinstance(g, int) and g == 0):
                    load_group(g, wo_w, wo_dram, wo_mm, 1, wo_in)
                if kk == per - 1 and not last:
                    load_group(g + 1, a_w, a_dram, tp_mm, G, a_in)
                    load_group(g + 1, v_w, v_dram, v_mm, 2, v_in)
                load_xs(2 * it + 3, 1, (2 * kk + 3) % NPAIR)
                load_tile(it)

            per = NPAIR // 2
            load_group(0, a_w, a_dram, tp_mm, G, a_in)
            load_xs(0, 0, 0)
            load_group(0, v_w, v_dram, v_mm, 2, v_in)
            load_group(0, wo_w, wo_dram, wo_mm, 1, wo_in)
            load_xs(1, 1, 1)
            load_tile(-1)
            sp.dma_start(bias[:], env["phi_b"].partition_broadcast(P)).then_inc(bias_in, 16)
            for it in range(per):
                iteration(it, it, 0)
            with sp.Fori(1, NG - 1) as g:
                for kk in range(per):
                    iteration(g * per + kk, kk, g)
            for kk in range(per):
                iteration(ITER - per + kk, kk, NG - 1, last=True)

        @block.tensor
        def _(pe):
            def transposes(v, q, ks):
                if ks[0] == 0:
                    pe.wait_ge(norm_done, v + 1)
                for k in ks:
                    n = 3 * v + k
                    bank = ps_t[:, (q + k) % 2, :]
                    wait(pe, t_out, n - 1)
                    for i in range(4):
                        if k == 2:
                            src = e1[q][:, i, P:S]
                        elif i % 2 == 0:
                            src = e0[q][:, 2 * k + i // 2, :]
                        else:
                            src = e1[q][:, 2 * k + i // 2, 0:P]
                        mm = pe.transpose(bank[:, i * P:(i + 1) * P], src, ident[:])
                    mm.then_inc(t_mm, 1)

            def scores(v, j, unit, ks):
                b, q = j % 2, (j // 2) % 2
                if b == 0 and ks[0] == 0:
                    pe.wait_ge(tp_hi, G * (unit + 1))
                    pe.wait_ge(tp_lo, G * (unit + 1))
                c0 = b * S
                for k in ks:
                    wait(pe, exp_done, 3 * (v - 1) + k + 1)
                    bank = ps_s[:, k, :]
                    if k == 0:
                        w, m = slice(c0, c0 + P), (slice(0, G), slice(c0, c0 + P))
                        masked, heads = bank.rearrange("p (h t) -> p h t", h=G), G
                        out = masked
                    else:
                        w, m = slice(c0 + P, c0 + S), (slice(2 * k - 2, 2 * k), slice(c0, c0 + S))
                        out = bank.rearrange("p (h t) -> p h t", h=2)
                        masked, heads = out[:, :, P:S], 2
                    product3(pe, out, xs[q][0][:, w], xs[q][1][:, w], tp[0][:, m[0], m[1]], tp[1][:, m[0], m[1]],
                             stop=False)
                    pe.matmul(masked, identb[:], mask[:, 0:heads, :], start=False, stop=True,
                              skip_group_check=True).then_inc(s_mm, 1)

            def logits(t, j):
                pe.wait_ge(fx_in, 32 * (t + 1))
                product3(pe, ps_tu[:, 0, :], fx[0][:], fx[1][:], phiT[0][:, j * BK:(j + 1) * BK],
                         phiT[1][:, j * BK:(j + 1) * BK]).then_inc(lg_mm, 1)

            def dispatch(t, j):
                if j == 0:
                    pe.wait_ge(fxn_in, 16 * (t + 1))
                pe.wait_ge(d_norm, 4 * t + j + 1)
                if not live(t + 1, NTT):
                    wait(pe, xt_out, 4 * t + j)
                pe.matmul(ps_tu[:, 1, :], fxn[:], bank_of(disp, t, j), start=True, stop=True).then_inc(xt_mm, 1)

            def output(v, j, unit, part):
                b, q = j % 2, (j // 2) % 2
                if part == 0 and b == 0:
                    pe.wait_ge(v_out, 2 * (unit + 1))
                    wait(pe, o_lo, unit)
                pe.wait_ge(t_out, 3 * v + part + 1)
                for i in range(G) if part == 2 else (2 * part, 2 * part + 1):
                    rows, cols = slice((i % 2) * DH, (i % 2 + 1) * DH), slice(i * DH, (i + 1) * DH)
                    if part < 2:
                        mm = pe.matmul(ps_o[rows, 0, b * S:(b + 1) * S], v_sb[q][:, 2 * b, cols],
                                       pT[:, part, (i % 2) * S:(i % 2 + 1) * S],
                                       start=(b == 0 and part == 0), stop=False, skip_group_check=True)
                    else:
                        mm = pe.matmul(ps_o[rows, 0, b * S + P:(b + 1) * S], v_sb[q][:, 2 * b + 1, cols],
                                       pT[:, 2, i * P:(i + 1) * P], start=False, stop=(i >= G - 2),
                                       skip_group_check=True)
                if part == 2:
                    mm.then_inc(av_mm, 1)

            def make_tp(unit, q, g, jobs=range(G)):
                for i in jobs:
                    if i == 0:
                        pe.wait_ge(a_in, 32 * (g + 1))
                        pe.wait_ge(xs_in[q], 32 * (unit // 2 + 1))
                    ring_free(i, unit)
                    product3(pe, ps_tu[:, i % 2, :], a_w[0][:, i * P:(i + 1) * P], a_w[1][:, i * P:(i + 1) * P],
                             xs[q][0][:], xs[q][1][:]).then_inc(tp_mm, 1)

            def make_v(unit, q, g, b):
                bank = 1 - b
                if b == 0:
                    pe.wait_ge(v_in, 32 * (g + 1))
                    wait(pe, xt_out, state["xt"])
                else:
                    wait(pe, lg_out, state["lg"])
                    wait(pe, wo_out, unit - 1)
                for i in range(2):
                    w = slice((2 * b + i) * P, (2 * b + i + 1) * P)
                    mm = product3(pe, ps_tu[:, bank, i * GV:(i + 1) * GV], xs[q][0][:, w], xs[q][1][:, w],
                                  v_w[0][:], v_w[1][:])
                mm.then_inc(v_mm, 1)

            def times_wo(unit):
                pe.wait_ge(wo_in, 32 * (unit // NPAIR + 1))
                pe.wait_ge(o_hi, unit + 1)
                pe.wait_ge(o_lo, unit + 1)
                wait(pe, lg_out, state["lg"])
                wait(pe, wo_out, unit)
                product3(pe, ps_tu[:, 0, :], wo_w[0][:], wo_w[1][:], o_t[0][:], o_t[1][:]).then_inc(wo_mm, 1)

            state = {}

            def ring_free(i, unit):
                if i == 0:
                    wait(pe, lg_out, state["lg"])
                elif i == 1:
                    wait(pe, xt_out, state["xt"])
                else:
                    pe.wait_ge(tp_hi, G * unit + i - 1)
                    pe.wait_ge(tp_lo, G * unit + i - 1)

            def step(it, j):
                v = 4 * it + j
                unit = 2 * it + j // 2
                if live(v - 2, NV):
                    transposes(v - 2, j % 2, (0, 1))
                made = unit if not isinstance(unit, int) else min(unit, NU - 1)
                if j % 2 == 0:
                    wait(pe, tp_hi, G * (made + 1) - 1)
                    wait(pe, tp_lo, G * (made + 1) - 1)
                    if live(it, NTT):
                        logits(it, j)
                if live(v, NV):
                    scores(v, j, unit, (0,))
                if live(v - 2, NV):
                    transposes(v - 2, j % 2, (2,))
                if live(v, NV):
                    scores(v, j, unit, (1,))
                if j % 2 == 1:
                    wait(pe, v_out, 2 * (made + 1))
                    if live(it, NTT):
                        logits(it, j)
                if live(v, NV):
                    scores(v, j, unit, (2,))
                if j % 2 == 0:
                    wait(pe, tp_hi, G * (made + 1))
                    wait(pe, tp_lo, G * (made + 1))
                if live(it - 1, NTT):
                    dispatch(it - 1, j)
                state["lg"] = 4 * it + j + 1 if live(it, NTT) else 4 * NTT
                state["xt"] = 4 * (it - 1) + j + 1 if live(it - 1, NTT) else 0

                def output_part(part):
                    if live(v - 2, NV):
                        output(v - 2, (j + 2) % 4, unit - 1, part)

                if j % 2 == 1:
                    for i in range(G):
                        if live(unit + 1, NU):
                            make_tp(unit + 1, (j // 2 + 1) % 2, (2 * it + j // 2 + 1) // NPAIR, (i,))
                        if i < 3:
                            output_part(i)
                else:
                    if live(unit - 2, NU):
                        times_wo(unit - 2)
                    output_part(0)
                    if live(unit, NU):
                        make_v(unit, (j // 2) % 2, (2 * it + j // 2) // NPAIR, 0)
                    output_part(1)
                    output_part(2)
                    if live(unit, NU):
                        make_v(unit, (j // 2) % 2, (2 * it + j // 2) // NPAIR, 1)

            state["lg"] = state["xt"] = 0
            make_tp(0, 0, 0)
            run(pe, step)

        @block.scalar
        def _(act):
            def transposed_out(v, q, ks):
                if live(v, NV):
                    for k in ks:
                        act.wait_ge(t_mm, 3 * v + k + 1)
                        wait(act, av_mm, v)
                        nc.scalar.activation(pT[:, k, :], ps_t[:, (q + k) % 2, :], ACT.Copy).then_inc(t_out, 1)

            def softmax_exp(v, j):
                q = j % 2
                wait(act, t_mm, 3 * (v - 1))
                for k in range(3):
                    act.wait_ge(max_done, 3 * v + k + 1)
                    if k == 0:
                        wait(act, inv_done, v - 1)
                    for i in range(G if k == 0 else 2):
                        h = i if k == 0 else 2 * (k - 1) + i
                        c = h if k == 0 else G + h
                        width = P if k == 0 else S
                        dst = e0[q][:, h, :] if k == 0 else e1[q][:, h, :]
                        ins = nc.scalar.activation(dst, ps_s[:, k, i * width:(i + 1) * width], ACT.Exp,
                                                   bias=neg_max[:, q, c:c + 1], accum_out=total[:, q, c:c + 1])
                    ins.then_inc(exp_done, 1)

            def step(it, j):
                v = 4 * it + j
                unit = 2 * it + j // 2
                if j % 2 == 0 and live(unit - 2, NU):
                    act.wait_ge(av_mm, 2 * (unit - 1))
                    wait(act, wo_mm, unit - 2)
                    nc.scalar.activation(o_t[0][:], ps_o[:, 0, :], ACT.Copy).then_inc(o_hi, 1)
                transposed_out(v - 2, j % 2, (0, 1))
                t, jj = step_before(it, j)
                if live(t, NTT):
                    act.wait_ge(d_sub, 4 * t + jj + 1)
                    bank = bank_of(disp, t, jj)
                    nc.scalar.activation(bank, bank, ACT.Exp).then_inc(d_exp, 1)
                transposed_out(v - 2, j % 2, (2,))
                if live(v, NV):
                    softmax_exp(v, j)
                for part in range(2):
                    if part == 1 and live(it - 1, NTT):
                        act.wait_ge(c_sub, 4 * (it - 1) + j + 1)
                        bank = bank_of(logit, it - 1, j)
                        nc.scalar.activation(bank, bank, ACT.Exp).then_inc(c_exp, 1)
                    two = (2 * part, 2 * part + 1)
                    if j % 2 == 1 and live(unit + 1, NU):
                        take_tp(unit + 1, two)
                    if j % 2 == 0 and live(unit, NU):
                        act.wait_ge(v_mm, 2 * unit + part + 1)
                        wait(act, av_mm, 2 * (unit - 1))
                        nc.scalar.activation(v_sb[(j // 2) % 2][:, two[0]:two[1] + 1, :],
                                             ps_tu[:, 1 - part, :].rearrange("p (t n) -> p t n", t=2),
                                             ACT.Copy).then_inc(v_out, 1)

            def take_tp(unit, jobs=range(G)):
                wait(act, s_mm, 6 * unit)
                for i in jobs:
                    act.wait_ge(tp_mm, G * unit + i + 1)
                    nc.scalar.activation(tp[0][:, i, :], ps_tu[:, i % 2, :], ACT.Copy).then_inc(tp_hi, 1)

            take_tp(0)
            run(act, step)

        @block.vector
        def _(dve):
            def bank_max(v, j, ks):
                q = j % 2
                for k in ks:
                    dve.wait_ge(s_mm, 3 * v + k + 1)
                    if k == 0:
                        wait(dve, exp_done, 3 * (v - 1))
                    heads = G if k == 0 else 2
                    c = 0 if k == 0 else G + 2 * (k - 1)
                    nc.vector.tensor_reduce(neg_max[:, q, c:c + heads],
                                            ps_s[:, k, :].rearrange("p (h t) -> p h t", h=heads),
                                            AX.X, ALU.max, negate=True).then_inc(max_done, 1)

            def take_tp_lo(unit, jobs=range(G)):
                for i in jobs:
                    dve.wait_ge(tp_hi, G * unit + i + 1)
                    nc.vector.tensor_tensor(tp[1][:, i, :], ps_tu[:, i % 2, :], f32(tp[0][:, i, :]),
                                            ALU.subtract).then_inc(tp_lo, 1)

            def step(it, j):
                v = 4 * it + j
                unit = 2 * it + j // 2
                t = it - 1
                if j % 2 == 0 and live(unit - 2, NU):
                    dve.wait_ge(o_hi, unit - 1)
                    nc.vector.tensor_tensor(o_t[1][:], ps_o[:, 0, :], f32(o_t[0][:]), ALU.subtract).then_inc(o_lo, 1)
                if j % 2 == 0 and live(it, NTT):
                    take_logits(it, j)
                if live(v, NV):
                    bank_max(v, j, (0, 1))
                if j % 2 == 1 and live(it, NTT):
                    take_logits(it, j)
                if live(v, NV):
                    bank_max(v, j, (2,))
                if live(it - 1, NTT):
                    t = it - 1
                    dve.wait_ge(xt_mm, 4 * t + j + 1)
                    wait(dve, xt_out, 4 * (t - 1) + j + 1)
                    acc = xt_acc[:, j * BK:(j + 1) * BK]
                    nc.vector.tensor_tensor(acc, ps_tu[:, 1, :], acc, ALU.add).then_inc(xt_out, 1)
                if j % 2 == 1:
                    dispatch_sums(*step_before(it, j))
                if j % 2 == 0 and live(unit - 2, NU):
                    dve.wait_ge(wo_mm, unit - 1)
                    wait(dve, wo_out, unit - 2)
                    o = o_acc[:, bass.ds(((unit - 2) % NPAIR) * PT, PT)]
                    nc.vector.tensor_tensor(o, ps_tu[:, 0, :], o, ALU.add).then_inc(wo_out, 1)

                def take_lo(i):
                    if j % 2 == 1 and live(unit + 1, NU):
                        take_tp_lo(unit + 1, (i,))

                take_lo(0)
                if live(it, NTT):
                    bank_maxima(it, j, (0,))
                take_lo(1)
                if live(it, NTT):
                    bank_maxima(it, j, (1,))
                if live(v, NV):
                    dve.wait_ge(exp_done, 3 * v + 3)
                    wait(dve, norm_done, v - 1)
                    nc.vector.reciprocal(inv[:, j % 2, :], total[:, j % 2, :]).then_inc(inv_done, 1)
                take_lo(2)
                take_lo(3)
                if live(it, NTT):
                    bank_maxima(it, j, (2,))
                if j % 2 == 0:
                    combine_sums(*step_before(it - 1, j))
                    dispatch_sums(*step_before(it, j))
                    combine_sums(it - 1, j)

            def carry_wait(c, j):
                nc.vector.memset(spare[:, 4 * c + j:4 * c + j + 1], 0.0)

            def take_logits(t, j):
                if isinstance(t, int) and t == 0 and j == 0:
                    dve.wait_ge(bias_in, 16)
                dve.wait_ge(lg_mm, 4 * t + j + 1)
                wait(dve, c_bank, 4 * (t - 2) + j + 1)
                nc.vector.tensor_tensor(bank_of(logit, t, j), ps_tu[:, 0, :], bias[:, j * BK:(j + 1) * BK],
                                        ALU.add).then_inc(lg_out, 1)

            def bank_maxima(t, j, parts):
                n = 4 * t + j
                bank = by_expert(bank_of(logit, t, j))
                if 0 in parts:
                    dve.wait_ge(lg_out, n + 1)
                    wait(dve, d_sub, n - 3)
                    wait(dve, m_done, t)
                    carry_wait(0, j)
                    nc.vector.tensor_reduce(gmax[:, j, :], bank, AX.X, ALU.max).then_inc(g_done, 1)
                if 1 in parts:
                    nc.vector.tensor_reduce(m_part[:, j, :], bank.rearrange("p e s -> p s e"), AX.X,
                                            ALU.max).then_inc(m_bank, 1)
                if 2 in parts and j == 3:
                    dve.wait_ge(m_bank, 4 * (t + 1))
                    carry_wait(1, j)
                    nc.vector.tensor_reduce(m_all[:, bass.ds(t * NP_, NP_)], m_part[:].rearrange("p j s -> p s j"),
                                            AX.X, ALU.max).then_inc(m_done, 1)

            def dispatch_sums(t, j):
                if live(t, NTT):
                    n = 4 * t + j
                    dve.wait_ge(d_exp, n + 1)
                    carry_wait(2, j)
                    nc.vector.tensor_reduce(dsum[:, j, :], by_expert(bank_of(disp, t, j)), AX.X,
                                            ALU.add).then_inc(d_sum, 1)
                    dve.wait_ge(d_sum, n + 1)
                    wait(dve, d_norm, n - 3)
                    nc.vector.reciprocal(dinv[:, j, :], dsum[:, j, :]).then_inc(d_inv, 1)

            def combine_sums(t, j):
                if not live(t, NTT):
                    return
                n = 4 * t + j
                dve.wait_ge(c_exp, n + 1)
                wait(dve, c_sum, t)
                carry_wait(3, j)
                nc.vector.tensor_reduce(c_part[:, j, :], by_expert(bank_of(logit, t, j)).rearrange("p e s -> p s e"),
                                        AX.X, ALU.add).then_inc(c_bank, 1)
                if j == 3:
                    dve.wait_ge(c_bank, n + 1)
                    carry_wait(4, j)
                    nc.vector.tensor_reduce(c_all[:, bass.ds(t * NP_, NP_)], c_part[:].rearrange("p j s -> p s j"),
                                            AX.X, ALU.add).then_inc(c_sum, 1)

            take_tp_lo(0)
            run(dve, step)
            combine_sums(NTT - 1, 3)

        @block.gpsimd
        def _(pool):
            def carry_wait(j):
                nc.gpsimd.tensor_tensor(pool_spare[:, j:j + 1], pool_spare[:, 4:5], pool_spare[:, 5:6], ALU.mult)

            nc.gpsimd.memset(pool_spare[:], 0.0)
            pool.drain()

            def step(it, j):
                v = 4 * it + j
                if live(it - 1, NTT):
                    t = it - 1
                    pool.wait_ge(m_done, t + 1)
                    bank = by_expert(bank_of(logit, t, j))
                    nc.gpsimd.tensor_tensor(bank, bank, m_all[:, bass.ds(t * NP_, NP_)].unsqueeze(1)
                                            .to_broadcast([P, EB, NP_]), ALU.subtract).then_inc(c_sub, 1)
                if live(it, NTT):
                    pool.wait_ge(g_done, 4 * it + j + 1)
                    wait(pool, xt_mm, 4 * (it - 2) + j + 1)
                    nc.gpsimd.tensor_tensor(by_expert(bank_of(disp, it, j)), by_expert(bank_of(logit, it, j)),
                                            gmax[:, j, :].unsqueeze(2).to_broadcast([P, EB, NP_]),
                                            ALU.subtract).then_inc(d_sub, 1)
                if live(v, NV):
                    q = j % 2
                    pool.wait_ge(inv_done, v + 1)
                    nc.gpsimd.tensor_tensor(e0[q][:], e0[q][:], inv[:, q, 0:G].unsqueeze(2)
                                            .to_broadcast([P, G, P]), ALU.mult)
                    nc.gpsimd.tensor_tensor(e1[q][:], e1[q][:], inv[:, q, G:2 * G].unsqueeze(2)
                                            .to_broadcast([P, G, S]), ALU.mult).then_inc(norm_done, 1)
                t, jj = step_before(it, j)
                if live(t, NTT):
                    pool.wait_ge(d_inv, 4 * t + jj + 1)
                    carry_wait(j)
                    bank = by_expert(bank_of(disp, t, jj))
                    nc.gpsimd.tensor_tensor(bank, bank, dinv[:, jj, :].unsqueeze(2).to_broadcast([P, EB, NP_]),
                                            ALU.mult).then_inc(d_norm, 1)

            run(pool, step)


def experts_phase(nc, env):
    with ExitStack() as ctx:
        def sb(name, shape, dt=F32):
            return ctx.enter_context(nc.sbuf_tensor(name, shape, dt))

        def sem(name):
            return ctx.enter_context(nc.semaphore(name))

        ew = sb("ew", [P, NE, D])
        eb = sb("eb", [P, NST, D])
        xslot = sb("xslot", [P, NST, D])
        xhT = sb("xhT", [P, NS_])
        stats = sb("stats2", [P, NST, 6])
        mv = sb("mv2", [P, NST, 2])
        var, root, quot, rstd, shift = (sb(n, [P, NST]) for n in ("var2", "root2", "quot2", "rstd2", "shift2"))
        ln_c = sb("ln_c", [P, NTT * NP_])
        lse_parts = sb("lse_parts", [P, NTT, 2, NP_], F32R)
        ps = ctx.enter_context(nc.psum_tensor("ps_e", [P, 8, BK], F32))

        ew_in, eb_in = sem("ew_in"), sem("eb_in")
        clip_done, xs_mm, xs_out, ln2, root_done, xhat, th = (
            sem(n) for n in ("clip_done", "xs_mm", "xs_out", "ln2", "root_done", "xhat", "th"))
        xh_mm, xh_out, y_mm, y_out, y_hi = (sem(n) for n in ("xh_mm", "xh_out", "y_mm", "y_out", "y_hi"))
        lnc_done, lse_done, lse_split, lt_mm, lt_out = (
            sem(n) for n in ("lnc_done", "lse_done", "lse_split", "lt_mm", "lt_out"))
        ident, xt_acc, m_all, c_all = env["ident"], env["xt_acc"], env["m_all"], env["c_all"]
        y_t, lseT = env["y_t"], env["lseT"]
        NQ = NST // 4
        NL = NTT // 4
        NDVE = NST // 2
        by_tile = ln_c[:].rearrange("p (t s) -> p t s", s=NP_)

        block = ctx.enter_context(nc.Block())

        @block.sync
        def _(sp):
            sp.dma_start(ew[:], env["expert_w"].rearrange("n d h -> d n h")).then_inc(ew_in, 16)
            per_tile = env["expert_b"].rearrange("(t r) h -> r t h", r=4)
            for r in range(4):
                sp.dma_start(eb[NP_ * r:NP_ * (r + 1)], per_tile[r].partition_broadcast(NP_)).then_inc(eb_in, 16)
            sp.wait_ge(ew_in, 16)
            sp.wait_ge(eb_in, 64)

        @block.scalar
        def _(act):
            nc.scalar.activation(ln_c[:], c_all[:], ACT.Ln).then_inc(lnc_done, 1)
            for c in range(NQ):
                act.wait_ge(xs_mm, c + 1)
                nc.scalar.activation(xslot[:, 4 * c:4 * c + 4, :], ps[:, c, :], ACT.Copy).then_inc(xs_out, 1)
            act.wait_ge(lse_done, 1)
            nc.scalar.activation(lse_parts[:, :, 0, :], by_tile, ACT.Copy).then_inc(lse_split, 1)
            act.wait_ge(ln2, 1)
            nc.scalar.activation(root[:], var[:], ACT.Sqrt).then_inc(root_done, 1)
            act.wait_ge(ln2, 7)
            for c in range(NQ):
                part = xslot[:, 4 * c:4 * c + 4, :]
                if 4 * c < NDVE:
                    act.wait_ge(xhat, c + 1)
                    nc.scalar.activation(part, part, ACT.Tanh).then_inc(th, 1)
                else:
                    for t in range(4 * c, 4 * c + 4):
                        ins = nc.scalar.activation(xslot[:, t, :], xslot[:, t, :], ACT.Tanh, bias=shift[:, t:t + 1],
                                                   scale=rstd[:, t:t + 1])
                    ins.then_inc(th, 1)
            for c in range(NQ):
                act.wait_ge(xh_mm, c + 1)
                nc.scalar.activation(xhT[:, c * BK:(c + 1) * BK], ps[:, c, :], ACT.Copy).then_inc(xh_out, 1)
            for c in range(NQ):
                act.wait_ge(y_out, c + 1)
                part = slice(4 * c, 4 * c + 4)
                nc.scalar.activation(y_t[0][:, part, :], eb[:, part, :], ACT.Copy).then_inc(y_hi, 1)

        @block.gpsimd
        def _(pool):
            pool.wait_ge(lnc_done, 1)
            nc.gpsimd.tensor_tensor(ln_c[:], ln_c[:], m_all[:], ALU.add).then_inc(lse_done, 1)
            pool.wait_ge(lse_split, 1)
            nc.gpsimd.tensor_tensor(lse_parts[:, :, 1, :], by_tile, f32(lse_parts[:, :, 0, :]),
                                    ALU.subtract).then_inc(lse_split, 1)

        @block.vector
        def _(dve):
            nc.vector.tensor_scalar(xt_acc[:], xt_acc[:], -33000.0, 65000.0, ALU.max, ALU.min).then_inc(clip_done, 1)
            for t in range(NST):
                if t % 4 == 0:
                    dve.wait_ge(xs_out, t // 4 + 1)
                nc.vector.bn_stats(stats[:, t, :], xslot[:, t, :])
            dve.drain()
            for t in range(NST):
                nc.vector.bn_aggr(mv[:, t, :], stats[:, t, :])
            dve.drain()
            nc.vector.tensor_scalar(var[:], mv[:, :, 1], EPS, None, ALU.add).then_inc(ln2, 1)
            dve.wait_ge(root_done, 1)
            nc.vector.reciprocal(quot[:], root[:]).then_inc(ln2, 1)
            dve.wait_ge(ln2, 2)
            nc.vector.tensor_tensor(quot[:], quot[:], var[:], ALU.mult).then_inc(ln2, 1)
            dve.wait_ge(ln2, 3)
            nc.vector.tensor_tensor(quot[:], quot[:], root[:], ALU.add).then_inc(ln2, 1)
            dve.wait_ge(ln2, 4)
            nc.vector.tensor_scalar(quot[:], quot[:], 0.5, None, ALU.mult).then_inc(ln2, 1)
            dve.wait_ge(ln2, 5)
            nc.vector.reciprocal(rstd[:], quot[:]).then_inc(ln2, 1)
            dve.wait_ge(ln2, 6)
            nc.vector.scalar_tensor_tensor(out=shift[:], in0=mv[:, :, 0], scalar=-1.0, in1=rstd[:], op0=ALU.mult,
                                           op1=ALU.mult).then_inc(ln2, 1)
            for t in range(NDVE):
                ins = nc.vector.tensor_scalar(xslot[:, t, :], xslot[:, t, :], mv[:, t, 0:1], rstd[:, t:t + 1],
                                              ALU.subtract, ALU.mult)
                if t % 4 == 3:
                    ins.then_inc(xhat, 1)
            for c in range(NL):
                dve.wait_ge(lt_mm, c + 1)
                nc.vector.tensor_copy(lseT[:, c * BK:(c + 1) * BK], ps[0:2 * NP_, 4 + c % 4, :]).then_inc(lt_out, 1)
            dve.wait_ge(eb_in, 64)
            for c in range(NQ + 1):
                if c < NQ:
                    dve.wait_ge(y_mm, c + 1)
                    part = slice(4 * c, 4 * c + 4)
                    nc.vector.tensor_tensor(eb[:, part, :], ps[:, 4 + c, :].rearrange("p (t h) -> p t h", t=4),
                                            eb[:, part, :], ALU.add).then_inc(y_out, 1)
                if c > 0:
                    dve.wait_ge(y_hi, c)
                    part = slice(4 * c - 4, 4 * c)
                    nc.vector.tensor_tensor(y_t[1][:, part, :], eb[:, part, :], f32(y_t[0][:, part, :]), ALU.subtract)

        @block.tensor
        def _(pe):
            pe.wait_ge(clip_done, 1)
            for t in range(NST):
                mm = pe.transpose(ps[:, t // 4, (t % 4) * P:(t % 4 + 1) * P], xt_acc[:, t * P:(t + 1) * P], ident[:])
                if t % 4 == 3:
                    mm.then_inc(xs_mm, 1)
            pe.wait_ge(lse_split, 2)
            for t in range(NTT):
                if t % 4 == 0 and t >= 16:
                    pe.wait_ge(lt_out, t // 4 - 3)
                mm = pe.transpose(ps[0:2 * NP_, 4 + (t // 4) % 4, (t % 4) * P:(t % 4 + 1) * P],
                                  f32(lse_parts[:, t, :, :].rearrange("p a b -> p (a b)")), ident[:])
                if t % 4 == 3:
                    mm.then_inc(lt_mm, 1)
            for t in range(NST):
                if t % 4 == 0:
                    pe.wait_ge(th, t // 4 + 1)
                mm = pe.transpose(ps[:, t // 4, (t % 4) * P:(t % 4 + 1) * P], xslot[:, t, :], ident[:])
                if t % 4 == 3:
                    mm.then_inc(xh_mm, 1)
            pe.wait_ge(ew_in, 16)
            pe.wait_ge(lt_out, NL)
            for t in range(NST):
                if t % 4 == 0:
                    pe.wait_ge(xh_out, t // 4 + 1)
                for r in range(4):
                    mm = pe.matmul(ps[NP_ * r:NP_ * (r + 1), 4 + t // 4, (t % 4) * P:(t % 4 + 1) * P],
                                   xhT[:, t * P + NP_ * r:t * P + NP_ * (r + 1)], ew[:, 4 * t + r, :],
                                   start=True, stop=True, skip_group_check=True)
                if t % 4 == 3:
                    mm.then_inc(y_mm, 1)


def combine_phase(nc, env):
    with ExitStack() as ctx:
        def sb(name, shape, dt=F32):
            return ctx.enter_context(nc.sbuf_tensor(name, shape, dt))

        def psum(name, banks):
            return ctx.enter_context(nc.psum_tensor(name, [P, banks, BK], F32))

        def sem(name):
            return ctx.enter_context(nc.semaphore(name))

        R = 4
        LAG = 2
        cT = sb("cT", [P, R, BK])
        c_hi, c_lo = (sb(n, [P, R, BK], F32R) for n in ("c_hi", "c_lo"))
        fin = sb("fin", [P, PT])
        xres = sb("xres", [P, 2, 4, D])
        res = sb("res", [P, 2, 4, D])
        ps_l, ps_y, ps_f = psum("ps_l", R), psum("ps_y", 2), psum("ps_f", 1)
        lt_mm, c_exp, c_low, y_mm, fin_done, f_mm, res_done = (
            sem(n) for n in ("lt2_mm", "c2_exp", "c2_low", "y2_mm", "fin_done", "f_mm", "res_done"))
        x_in = [sem("x_in0"), sem("x_in1")]
        stored = [sem("stored0"), sem("stored1")]
        ident, xT, phiT, nsel, lseT = env["ident"], env["xT"], env["phiT"], env["nsel"], env["lseT"]
        y_t, phibT, o_acc = env["y_t"], env["phibT"], env["o_acc"]
        x_pair = env["x"].rearrange("(n t p) d -> n p t d", p=P, t=4)
        out_pair = env["out"].rearrange("(n t p) d -> n p t d", p=P, t=4)

        block = ctx.enter_context(nc.Block())

        @block.sync
        def _(sp):
            for p in range(NPAIR):
                wait(sp, res_done, p - 1)
                sp.dma_start(xres[:, p % 2], x_pair[p]).then_inc(x_in[p % 2], 16)

        @block.gpsimd
        def _(pool):
            for p in range(NPAIR):
                pool.wait_ge(res_done, p + 1)
                pool.dma_start(out_pair[p], res[:, p % 2]).then_inc(stored[p % 2], 16)
            for q in range(2):
                pool.wait_ge(stored[q], 16 * NPAIR // 2)

        @block.tensor
        def _(pe):
            def untranspose(p):
                pe.wait_ge(fin_done, p + 1)
                wait(pe, res_done, p)
                for i in range(4):
                    mm = pe.transpose(ps_f[:, 0, i * P:(i + 1) * P], fin[:, i * P:(i + 1) * P], ident[:])
                mm.then_inc(f_mm, 1)

            def logits_t(p, st):
                n = NST * p + st
                w, tok = slice(st * P, (st + 1) * P), bass.ds(p * PT, PT)
                wait(pe, c_exp, n - R + 1)
                product3(pe, ps_l[:, st % R, :], phiT[0][:, w], phiT[1][:, w], xT[0][:, tok], xT[1][:, tok],
                         stop=False)
                pe.matmul(ps_l[:, st % R, :], nsel[:], lseT[:, tok], start=False, stop=True,
                          skip_group_check=True).then_inc(lt_mm, 1)

            def mix(p, q, st):
                pe.wait_ge(c_low, NST * p + st + 1)
                if st == 0:
                    wait(pe, fin_done, p - 1)
                product3(pe, ps_y[:, q, :], y_t[0][:, st, :], y_t[1][:, st, :], c_hi[:, st % R, :],
                         c_lo[:, st % R, :], start=(st == 0), stop=(st == NST - 1)).then_inc(y_mm, 1)

            def pair(p, q):
                for st in range(NST):
                    logits_t(p, st)
                    if st >= LAG:
                        mix(p, q, st - LAG)
                    elif live(p - 1, NPAIR):
                        mix(p - 1, 1 - q, NST + st - LAG)
                    if st == 6 and live(p - 1, NPAIR):
                        untranspose(p - 1)

            pair(0, 0)
            pair(1, 1)
            with pe.Fori(1, NPAIR // 2) as pp:
                for q in range(2):
                    pair(2 * pp + q, q)
            for st in range(NST - LAG, NST):
                mix(NPAIR - 1, 1, st)
            untranspose(NPAIR - 1)

        @block.scalar
        def _(act):
            def pair(p):
                for st in range(NST):
                    act.wait_ge(lt_mm, NST * p + st + 1)
                    wait(act, y_mm, NST * p + st - R + 1)
                    nc.scalar.activation(c_hi[:, st % R, :], ps_l[:, st % R, :], ACT.Exp, bias=phibT[:, st:st + 1])
                    nc.scalar.activation(cT[:, st % R, :], ps_l[:, st % R, :], ACT.Exp,
                                         bias=phibT[:, st:st + 1]).then_inc(c_exp, 1)

            pair(0)
            with act.Fori(1, NPAIR) as p:
                pair(p)

        @block.vector
        def _(dve):
            def add_x(p):
                dve.wait_ge(f_mm, p + 1)
                dve.wait_ge(x_in[p % 2], 16 * (p // 2 + 1))
                wait(dve, stored[p % 2], 16 * (p // 2))
                nc.vector.tensor_tensor(res[:, p % 2], ps_f[:, 0, :].rearrange("p (t d) -> p t d", t=4),
                                        xres[:, p % 2], ALU.add).then_inc(res_done, 1)

            def low_parts(p, tiles):
                for st in tiles:
                    dve.wait_ge(c_exp, NST * p + st + 1)
                    wait(dve, y_mm, NST * p + st - R + 1)
                    nc.vector.tensor_tensor(c_lo[:, st % R, :], cT[:, st % R, :], f32(c_hi[:, st % R, :]),
                                            ALU.subtract).then_inc(c_low, 1)

            def finish(p):
                dve.wait_ge(y_mm, NST * (p + 1))
                wait(dve, f_mm, p)
                nc.vector.tensor_tensor(fin[:], ps_y[:, p % 2, :], o_acc[:, p * PT:(p + 1) * PT],
                                        ALU.add).then_inc(fin_done, 1)

            EARLY = 3
            for p in range(NPAIR + 1):
                if p < NPAIR:
                    low_parts(p, range(EARLY))
                if p > 0:
                    finish(p - 1)
                if p < NPAIR:
                    low_parts(p, range(EARLY, 8))
                if p > 0:
                    add_x(p - 1)
                if p < NPAIR:
                    low_parts(p, range(8, NST))


def build(nc, x, wq, wk, wv, wo, lq1, lk1, lq2, lk2, phi_w, phi_b, expert_w, expert_b, out):
    with ExitStack() as ctx:
        def sb(name, shape, dt=F32):
            return ctx.enter_context(nc.sbuf_tensor(name, shape, dt))

        env = dict(x=x.rearrange("b s d -> (b s) d"), wq=wq, wk=wk, wv=wv, wo=wo, lq1=lq1, lk1=lk1, lq2=lq2, lk2=lk2,
                   phi_w=phi_w, phi_b=phi_b, expert_w=expert_w, expert_b=expert_b,
                   out=out.rearrange("b s d -> (b s) d"))
        env["a_dram"] = nc.dram_tensor("a_scratch", [NG, 2, P, G * P], F32, kind="Internal").ap()
        env["v_dram"] = nc.dram_tensor("v_scratch", [NG, 2, P, GV], F32, kind="Internal").ap()
        env["wo_dram"] = nc.dram_tensor("wo_scratch", [NG, 2, P, D], F32, kind="Internal").ap()
        env["ident"] = sb("ident", [P, P])
        env["identb"] = sb("identb", [P, P], BF16)
        env["mask"] = sb("mask", [P, G, P], BF16)
        env["xn"] = sb("xn", [P, NTT, D])
        env["xT"] = [sb(f"xT{h}", [P, NT], F32R) for h in range(2)]
        env["phiT"] = [sb(f"phiT{h}", [P, NS_], F32R) for h in range(2)]
        env["phibT"] = sb("phibT", [P, NST])
        env["nsel_f"] = sb("nsel_f", [2 * NP_, P])
        env["nsel"] = sb("nsel", [2 * NP_, P], F32R)
        env["o_acc"] = sb("o_acc", [P, NT])
        env["xt_acc"] = sb("xt_acc", [P, NS_])
        env["m_all"] = sb("m_all", [P, NTT * NP_])
        env["c_all"] = sb("c_all", [P, NTT * NP_])
        setup_phase(nc, env)
        main_phase(nc, env)
        env["y_t"] = [sb(f"y_t{h}", [P, NST, D], F32R) for h in range(2)]
        env["lseT"] = sb("lseT", [2 * NP_, NT], F32R)
        experts_phase(nc, env)
        combine_phase(nc, env)


_INS = ["L0_attn_x", "L0_attn_Wq", "L0_attn_Wk", "L0_attn_Wv", "L0_attn_Wo", "L0_attn_lq1", "L0_attn_lk1",
        "L0_attn_lq2", "L0_attn_lk2", "L0_ffn_phi_w", "L0_ffn_phi_b", "L0_ffn_expert_w", "L0_ffn_expert_b"]


def kernel(**inputs):
    import concourse.bacc as bacc
    from concourse.bass_utils import run_bass_kernel_spmd as run

    nc = bacc.Bacc("TRN2", target_bir_lowering=False, num_devices=1)
    arrays, args = {}, []
    for name in _INS:
        a = np.ascontiguousarray(inputs[name])
        arrays[f"in_{name}"] = a
        args.append(nc.dram_tensor(f"in_{name}", a.shape, mybir.dt.from_np(a.dtype), kind="ExternalInput").ap())
    out = nc.dram_tensor("out_dram", (NB, S, D), F32, kind="ExternalOutput").ap()
    build(nc, *args, out)
    r = run(nc, [arrays], core_ids=[0])
    return r.results[0]["out_dram"]
```
